# Optimizing a Trainium2 kernel written in Bass

```python
import numpy as np
import jax
import jax.numpy as jnp

def _softmax(x, axis=-1):
    return jax.nn.softmax(x, axis=axis)

def _gelu(x):
    return jax.nn.gelu(x, approximate=True)

def _silu(x):
    return jax.nn.silu(x)

def _sigmoid(x):
    return jax.nn.sigmoid(x)

def _layernorm(x, axis=-1, eps=1e-05):
    m = jnp.mean(x, axis=axis, keepdims=True)
    v = jnp.var(x, axis=axis, keepdims=True)
    return (x - m) / jnp.sqrt(v + eps)

def _scatter_add(tgt, idx, src, axis=0):
    return tgt.at[idx].add(src)

def _segment_sum(src, seg, n):
    return jax.ops.segment_sum(src, seg, n)
kernel_name = 'mk_gnn_resnorm_d4_gnn_r8_89de73'

def setup_inputs(seed: int=0):
    np.random.seed(seed)
    _w = jnp.asarray

    def _rec_inputs():
        import jax
        import jax.numpy as jnp
        _gk = jax.random.key(seed)
        x = -3.713e-05 + 0.1 * jax.random.normal(jax.random.fold_in(_gk, 1), (12500, 64), jnp.float32)
        src = jax.random.randint(jax.random.fold_in(_gk, 2), (200000,), 0, 12500, jnp.int32)
        dst = jax.random.randint(jax.random.fold_in(_gk, 3), (200000,), 0, 12500, jnp.int32)
        _o = jnp.argsort(dst, stable=True)
        src = src[_o]
        dst = dst[_o]
        edge_type_33 = jax.random.randint(jax.random.fold_in(_gk, 12), (200000,), 0, 33, jnp.int32)
        edge_weight1 = 9.9816e-05 + 0.999782 * jax.random.normal(jax.random.fold_in(_gk, 13), (200000, 1), jnp.float32)
        return (x, src, dst, edge_type_33, edge_weight1)
    x, src, dst, edge_type_33, edge_weight1 = _rec_inputs()

    def _L0_gnn_setup():
        import jax, jax.numpy as jnp
        import numpy as np
        MIN_NORM = 1e-15
        BALL_EPS = 0.004
        RES_LAMBDA = 0.5
        N_HOPS = 2

        def _artanh(x):
            x = jnp.clip(x, -1.0 + 1e-07, 1.0 - 1e-07)
            return 0.5 * jnp.log((1.0 + x) / (1.0 - x))

        def _norm(x):
            return jnp.clip(jnp.linalg.norm(x, axis=-1, keepdims=True), MIN_NORM, None)

        def expmap0(u):
            n = _norm(u)
            return jnp.tanh(n) * u / n

        def mobius_add(x, y):
            x2 = jnp.sum(x * x, axis=-1, keepdims=True)
            y2 = jnp.sum(y * y, axis=-1, keepdims=True)
            xy = jnp.sum(x * y, axis=-1, keepdims=True)
            num = (1.0 + 2.0 * xy + y2) * x + (1.0 - x2) * y
            den = jnp.clip(1.0 + 2.0 * xy + x2 * y2, MIN_NORM, None)
            return num / den

        def expmap(u, p):
            lam = 2.0 / jnp.clip(1.0 - jnp.sum(p * p, axis=-1, keepdims=True), MIN_NORM, None)
            n = _norm(u)
            second = jnp.tanh(0.5 * lam * n) * u / n
            return mobius_add(p, second)

        def logmap(y, p):
            sub = mobius_add(-p, y)
            n = _norm(sub)
            lam = 2.0 / jnp.clip(1.0 - jnp.sum(p * p, axis=-1, keepdims=True), MIN_NORM, None)
            return 2.0 / lam * _artanh(n) * sub / n

        def project(x):
            n = _norm(x)
            maxnorm = 1.0 - BALL_EPS
            return jnp.where(n > maxnorm, x / n * maxnorm, x)

        def _l2_normalize(x, eps=1e-12):
            return x / jnp.clip(jnp.linalg.norm(x, axis=-1, keepdims=True), eps, None)

        def _agg(entity_emb, relation_emb, head, tail, relation_type):
            n_entities = entity_emb.shape[0]
            head_emb = entity_emb[head]
            tail_emb = entity_emb[tail]
            rel_emb = relation_emb[relation_type]
            ricci = _l2_normalize(tail_emb + rel_emb)
            hyper_head = expmap0(head_emb)
            hyper_tail = expmap(tail_emb, hyper_head)
            hyper_rel = expmap(rel_emb, hyper_head)
            res = project(mobius_add(hyper_tail, hyper_rel))
            res = logmap(res, hyper_head) + ricci * 1e-07
            res = jax.nn.relu(res)
            sums = jnp.zeros((n_entities, res.shape[-1]), res.dtype).at[head].add(res)
            counts = jnp.zeros((n_entities,), res.dtype).at[head].add(1.0)
            return sums / jnp.clip(counts, 1.0, None)[:, None]
        key = jax.random.key(seed)
        k1, k2, k3, k4, k5 = jax.random.split(key, 5)
        n_entities, n_relations, latdim, n_edges = (25000, 32, 64, 125000)
        entity_emb = 0.1 * jax.random.normal(k1, (n_entities, latdim), dtype=jnp.float32)
        relation_emb = 0.1 * jax.random.normal(k2, (n_relations, latdim), dtype=jnp.float32)
        head = jax.random.randint(k3, (n_edges,), 0, n_entities)
        tail = jax.random.randint(k4, (n_edges,), 0, n_entities)
        edge_index = jnp.stack([head, tail], axis=0).astype(jnp.int64)
        edge_type = jax.random.randint(k5, (n_edges,), 1, n_relations + 1).astype(jnp.int64)
        return {'entity_emb': entity_emb, 'relation_emb': relation_emb, 'edge_index': edge_index, 'edge_type': edge_type}
    _L0_gnn_all = _L0_gnn_setup()
    _L0_gnn_in = {k: v for k, v in _L0_gnn_all.items() if k in ('relation_emb',)}
    del _L0_gnn_all

    def _L1_gnn_setup():
        import jax, jax.numpy as jnp
        import numpy as np
        N = 12500
        E = 156250
        H = 64
        T = 2

        def _gru_cell(inp, h, Wih, bih, Whh, bhh):
            gi = inp @ Wih.T + bih
            gh = h @ Whh.T + bhh
            i_r, i_z, i_n = jnp.split(gi, 3, axis=1)
            h_r, h_z, h_n = jnp.split(gh, 3, axis=1)
            r = jax.nn.sigmoid(i_r + h_r)
            z = jax.nn.sigmoid(i_z + h_z)
            n = jnp.tanh(i_n + r * h_n)
            return (1.0 - z) * n + z * h
        key = jax.random.key(seed)
        ks = jax.random.split(key, 10)
        s = 0.1
        return {'x': jax.random.normal(ks[0], (N, H), dtype=jnp.float32), 'edge_index': jax.random.randint(ks[1], (2, E), 0, N, dtype=jnp.int64), 'edge_attr': jax.random.normal(ks[2], (E, 1), dtype=jnp.float32), 'msg_W': jax.random.normal(ks[3], (T, H, 2 * H + 1), dtype=jnp.float32) * s, 'msg_b': jax.random.normal(ks[4], (T, H), dtype=jnp.float32) * s, 'gru_Wih': jax.random.normal(ks[5], (T, 3 * H, H), dtype=jnp.float32) * s, 'gru_bih': jax.random.normal(ks[6], (T, 3 * H), dtype=jnp.float32) * s, 'gru_Whh': jax.random.normal(ks[7], (T, 3 * H, H), dtype=jnp.float32) * s, 'gru_bhh': jax.random.normal(ks[8], (T, 3 * H), dtype=jnp.float32) * s}
    _L1_gnn_all = _L1_gnn_setup()
    _L1_gnn_in = {k: v for k, v in _L1_gnn_all.items() if k in ('msg_W', 'msg_b', 'gru_Wih', 'gru_bih', 'gru_Whh', 'gru_bhh')}
    del _L1_gnn_all

    def _L2_gnn_setup():
        import jax, jax.numpy as jnp
        import numpy as np
        HIDDEN = 16

        def _sage_conv(h, src, dst, inv_deg, W_l, b_l, W_r):
            N = h.shape[0]
            agg = jax.ops.segment_sum(h[src], dst, num_segments=N) * inv_deg
            return agg @ W_l + b_l + h @ W_r
        key = jax.random.key(seed)
        ks = jax.random.split(key, 8)
        N, E, D_IN, D_OUT = (12500, 200000, 64, 64)
        x = jax.random.normal(ks[0], (N, D_IN), dtype=jnp.float32)
        edge_index = jax.random.randint(ks[1], (2, E), 0, N, dtype=jnp.int64)

        def glorot(k, shape):
            lim = float(np.sqrt(6.0 / (shape[0] + shape[1])))
            return jax.random.uniform(k, shape, jnp.float32, -lim, lim)
        return {'x': x, 'edge_index': edge_index, 'W1_l': glorot(ks[2], (D_IN, HIDDEN)), 'b1': jnp.zeros((HIDDEN,), jnp.float32), 'W1_r': glorot(ks[3], (D_IN, HIDDEN)), 'W2_l': glorot(ks[4], (HIDDEN, D_OUT)), 'b2': jnp.zeros((D_OUT,), jnp.float32), 'W2_r': glorot(ks[5], (HIDDEN, D_OUT))}
    _L2_gnn_all = _L2_gnn_setup()
    _L2_gnn_in = {k: v for k, v in _L2_gnn_all.items() if k in ('W1_l', 'b1', 'W1_r', 'W2_l', 'b2', 'W2_r')}
    del _L2_gnn_all

    def _L3_gnn_setup():
        import jax, jax.numpy as jnp
        import numpy as np
        N_NODES = 12500
        N_EDGES = 200000
        IN_C, HID_C, OUT_C = (64, 128, 64)

        def _glorot(key, shape):
            fan_in, fan_out = (shape[1], shape[0])
            s = jnp.sqrt(6.0 / (fan_in + fan_out))
            return jax.random.uniform(key, shape, jnp.float32, -s, s)

        def _sage_conv(x, src, dst, W_l, b, W_r, n_nodes):
            msg = x[src]
            agg = jax.ops.segment_sum(msg, dst, num_segments=n_nodes)
            cnt = jax.ops.segment_sum(jnp.ones((src.shape[0],), x.dtype), dst, num_segments=n_nodes)
            agg = agg / jnp.maximum(cnt, 1.0)[:, None]
            return agg @ W_l.T + b + x @ W_r.T
        key = jax.random.key(seed)
        ks = jax.random.split(key, 8)
        x = jax.random.normal(ks[0], (N_NODES, IN_C), jnp.float32)
        edge_index = jax.random.randint(ks[1], (2, N_EDGES), 0, N_NODES, jnp.int64)
        return {'x': x, 'edge_index': edge_index, 'W1_l': _glorot(ks[2], (HID_C, IN_C)), 'b1': jnp.zeros((HID_C,), jnp.float32), 'W1_r': _glorot(ks[3], (HID_C, IN_C)), 'W2_l': _glorot(ks[4], (OUT_C, HID_C)), 'b2': jnp.zeros((OUT_C,), jnp.float32), 'W2_r': _glorot(ks[5], (OUT_C, HID_C))}
    _L3_gnn_all = _L3_gnn_setup()
    _L3_gnn_in = {k: v for k, v in _L3_gnn_all.items() if k in ('W1_l', 'b1', 'W1_r', 'W2_l', 'b2', 'W2_r')}
    del _L3_gnn_all
    return {'x': x, 'src': src, 'dst': dst, 'edge_type_33': edge_type_33, 'edge_weight1': edge_weight1, 'L0_gnn_relation_emb': _L0_gnn_in['relation_emb'], 'L1_gnn_msg_W': _L1_gnn_in['msg_W'], 'L1_gnn_msg_b': _L1_gnn_in['msg_b'], 'L1_gnn_gru_Wih': _L1_gnn_in['gru_Wih'], 'L1_gnn_gru_bih': _L1_gnn_in['gru_bih'], 'L1_gnn_gru_Whh': _L1_gnn_in['gru_Whh'], 'L1_gnn_gru_bhh': _L1_gnn_in['gru_bhh'], 'L2_gnn_W1_l': _L2_gnn_in['W1_l'], 'L2_gnn_b1': _L2_gnn_in['b1'], 'L2_gnn_W1_r': _L2_gnn_in['W1_r'], 'L2_gnn_W2_l': _L2_gnn_in['W2_l'], 'L2_gnn_b2': _L2_gnn_in['b2'], 'L2_gnn_W2_r': _L2_gnn_in['W2_r'], 'L3_gnn_W1_l': _L3_gnn_in['W1_l'], 'L3_gnn_b1': _L3_gnn_in['b1'], 'L3_gnn_W1_r': _L3_gnn_in['W1_r'], 'L3_gnn_W2_l': _L3_gnn_in['W2_l'], 'L3_gnn_b2': _L3_gnn_in['b2'], 'L3_gnn_W2_r': _L3_gnn_in['W2_r']}

def reference(x, src, dst, edge_type_33, edge_weight1, L0_gnn_relation_emb, L1_gnn_msg_W, L1_gnn_msg_b, L1_gnn_gru_Wih, L1_gnn_gru_bih, L1_gnn_gru_Whh, L1_gnn_gru_bhh, L2_gnn_W1_l, L2_gnn_b1, L2_gnn_W1_r, L2_gnn_W2_l, L2_gnn_b2, L2_gnn_W2_r, L3_gnn_W1_l, L3_gnn_b1, L3_gnn_W1_r, L3_gnn_W2_l, L3_gnn_b2, L3_gnn_W2_r):
    import jax
    import jax.numpy as jnp

    def _L0_gnn_ref(entity_emb, relation_emb, edge_index, edge_type):
        import jax, jax.numpy as jnp
        import numpy as np
        MIN_NORM = 1e-15
        BALL_EPS = 0.004
        RES_LAMBDA = 0.5
        N_HOPS = 2

        def _artanh(x):
            x = jnp.clip(x, -1.0 + 1e-07, 1.0 - 1e-07)
            return 0.5 * jnp.log((1.0 + x) / (1.0 - x))

        def _norm(x):
            return jnp.clip(jnp.linalg.norm(x, axis=-1, keepdims=True), MIN_NORM, None)

        def expmap0(u):
            n = _norm(u)
            return jnp.tanh(n) * u / n

        def mobius_add(x, y):
            x2 = jnp.sum(x * x, axis=-1, keepdims=True)
            y2 = jnp.sum(y * y, axis=-1, keepdims=True)
            xy = jnp.sum(x * y, axis=-1, keepdims=True)
            num = (1.0 + 2.0 * xy + y2) * x + (1.0 - x2) * y
            den = jnp.clip(1.0 + 2.0 * xy + x2 * y2, MIN_NORM, None)
            return num / den

        def expmap(u, p):
            lam = 2.0 / jnp.clip(1.0 - jnp.sum(p * p, axis=-1, keepdims=True), MIN_NORM, None)
            n = _norm(u)
            second = jnp.tanh(0.5 * lam * n) * u / n
            return mobius_add(p, second)

        def logmap(y, p):
            sub = mobius_add(-p, y)
            n = _norm(sub)
            lam = 2.0 / jnp.clip(1.0 - jnp.sum(p * p, axis=-1, keepdims=True), MIN_NORM, None)
            return 2.0 / lam * _artanh(n) * sub / n

        def project(x):
            n = _norm(x)
            maxnorm = 1.0 - BALL_EPS
            return jnp.where(n > maxnorm, x / n * maxnorm, x)

        def _l2_normalize(x, eps=1e-12):
            return x / jnp.clip(jnp.linalg.norm(x, axis=-1, keepdims=True), eps, None)

        def _agg(entity_emb, relation_emb, head, tail, relation_type):
            n_entities = entity_emb.shape[0]
            head_emb = entity_emb[head]
            tail_emb = entity_emb[tail]
            rel_emb = relation_emb[relation_type]
            ricci = _l2_normalize(tail_emb + rel_emb)
            hyper_head = expmap0(head_emb)
            hyper_tail = expmap(tail_emb, hyper_head)
            hyper_rel = expmap(rel_emb, hyper_head)
            res = project(mobius_add(hyper_tail, hyper_rel))
            res = logmap(res, hyper_head) + ricci * 1e-07
            res = jax.nn.relu(res)
            sums = jnp.zeros((n_entities, res.shape[-1]), res.dtype).at[head].add(res)
            counts = jnp.zeros((n_entities,), res.dtype).at[head].add(1.0)
            return sums / jnp.clip(counts, 1.0, None)[:, None]
        head, tail = (edge_index[0], edge_index[1])
        relation_type = edge_type - 1
        entity_res_emb = entity_emb
        e = entity_emb
        for _ in range(N_HOPS):
            e = _agg(e, relation_emb, head, tail, relation_type)
            e = _l2_normalize(e)
            entity_res_emb = RES_LAMBDA * entity_res_emb + e
        return entity_res_emb

    def _L1_gnn_ref(x, edge_index, edge_attr, msg_W, msg_b, gru_Wih, gru_bih, gru_Whh, gru_bhh):
        import jax, jax.numpy as jnp
        import numpy as np
        N = 12500
        E = 156250
        H = 64
        T = 2

        def _gru_cell(inp, h, Wih, bih, Whh, bhh):
            gi = inp @ Wih.T + bih
            gh = h @ Whh.T + bhh
            i_r, i_z, i_n = jnp.split(gi, 3, axis=1)
            h_r, h_z, h_n = jnp.split(gh, 3, axis=1)
            r = jax.nn.sigmoid(i_r + h_r)
            z = jax.nn.sigmoid(i_z + h_z)
            n = jnp.tanh(i_n + r * h_n)
            return (1.0 - z) * n + z * h
        row, col = (edge_index[0], edge_index[1])
        num_rounds = msg_W.shape[0]
        for t in range(num_rounds):
            src = x[row]
            dest = x[col]
            m_input = jnp.concatenate([dest, src, edge_attr], axis=1)
            messages = m_input @ msg_W[t].T + msg_b[t]
            agg = jax.ops.segment_sum(messages, row, num_segments=x.shape[0])
            x = _gru_cell(agg, x, gru_Wih[t], gru_bih[t], gru_Whh[t], gru_bhh[t])
        return x

    def _L2_gnn_ref(x, edge_index, W1_l, b1, W1_r, W2_l, b2, W2_r):
        import jax, jax.numpy as jnp
        import numpy as np
        HIDDEN = 16

        def _sage_conv(h, src, dst, inv_deg, W_l, b_l, W_r):
            N = h.shape[0]
            agg = jax.ops.segment_sum(h[src], dst, num_segments=N) * inv_deg
            return agg @ W_l + b_l + h @ W_r
        src, dst = (edge_index[0], edge_index[1])
        N = x.shape[0]
        deg = jax.ops.segment_sum(jnp.ones_like(dst, dtype=x.dtype), dst, num_segments=N)
        inv_deg = (1.0 / jnp.maximum(deg, 1.0))[:, None]
        h = jax.nn.relu(_sage_conv(x, src, dst, inv_deg, W1_l, b1, W1_r))
        out = _sage_conv(h, src, dst, inv_deg, W2_l, b2, W2_r)
        return out

    def _L3_gnn_ref(x, edge_index, W1_l, b1, W1_r, W2_l, b2, W2_r):
        import jax, jax.numpy as jnp
        import numpy as np
        N_NODES = 12500
        N_EDGES = 200000
        IN_C, HID_C, OUT_C = (64, 128, 64)

        def _glorot(key, shape):
            fan_in, fan_out = (shape[1], shape[0])
            s = jnp.sqrt(6.0 / (fan_in + fan_out))
            return jax.random.uniform(key, shape, jnp.float32, -s, s)

        def _sage_conv(x, src, dst, W_l, b, W_r, n_nodes):
            msg = x[src]
            agg = jax.ops.segment_sum(msg, dst, num_segments=n_nodes)
            cnt = jax.ops.segment_sum(jnp.ones((src.shape[0],), x.dtype), dst, num_segments=n_nodes)
            agg = agg / jnp.maximum(cnt, 1.0)[:, None]
            return agg @ W_l.T + b + x @ W_r.T
        src, dst = (edge_index[0], edge_index[1])
        n = x.shape[0]
        h = _sage_conv(x, src, dst, W1_l, b1, W1_r, n)
        h = jax.nn.relu(h)
        out = _sage_conv(h, src, dst, W2_l, b2, W2_r, n)
        return jnp.squeeze(out)
    edge_index = jnp.stack([src, dst])
    x = _layernorm(x + _L0_gnn_ref(x, L0_gnn_relation_emb, edge_index, edge_type_33), axis=-1)
    x = _layernorm(x + _L1_gnn_ref(x, edge_index, edge_weight1, L1_gnn_msg_W, L1_gnn_msg_b, L1_gnn_gru_Wih, L1_gnn_gru_bih, L1_gnn_gru_Whh, L1_gnn_gru_bhh), axis=-1)
    x = _layernorm(x + _L2_gnn_ref(x, edge_index, L2_gnn_W1_l, L2_gnn_b1, L2_gnn_W1_r, L2_gnn_W2_l, L2_gnn_b2, L2_gnn_W2_r), axis=-1)
    x = _layernorm(x + _L3_gnn_ref(x, edge_index, L3_gnn_W1_l, L3_gnn_b1, L3_gnn_W1_r, L3_gnn_W2_l, L3_gnn_b2, L3_gnn_W2_r), axis=-1)
    return x

_drawn_inputs = setup_inputs


def setup_inputs(seed=0):
    import zlib

    import numpy as np

    out = dict(_drawn_inputs(seed))
    spreads = {'L2_gnn_b1': (0.0, 0.1),
     'L2_gnn_b2': (0.0, 0.1),
     'L3_gnn_b1': (0.0, 0.1),
     'L3_gnn_b2': (0.0, 0.1)}
    factors = {'L1_gnn_gru_bhh': 2.896}
    for name, (base, spread) in spreads.items():
        noise = np.random.default_rng([zlib.crc32(name.encode()), seed]).standard_normal(out[name].shape)
        drawn = base * np.exp(spread * noise) if base else spread * noise
        out[name] = jnp.asarray(drawn.astype(out[name].dtype))
    for name, factor in factors.items():
        out[name] = (out[name] * factor).astype(out[name].dtype)
    return out
```

```python
import concourse.bass as bass
from concourse import mybir
from contextlib import ExitStack

FP32 = mybir.dt.float32
BF16 = mybir.dt.bfloat16
I32 = mybir.dt.int32
I16 = mybir.dt.int16
ALU = mybir.AluOpType
ACT = mybir.ActivationFunctionType
AX = mybir.AxisListType

P = 128
D = 64
N = 12500
NB = -(-N // P)
LAST = N - (NB - 1) * P
E = 200000
EP, EC = 125, E // 125
R = 32
G = 32
QG = G // 4
GROUPS = 52
TILES = GROUPS * G
assert TILES >= E // P + NB and GROUPS % 2 == 0
ITERS = GROUPS // 2
W = D + 2
TW = 100
C_EE, C_NE, C_A, C_PP = 96, 97, 98, 99
RW = D + 2
CH = 5
HC = 40
NCH = HC // CH
GITERS = EC // HC // 2
KB = 7
NITERS = NB // KB
assert NITERS * KB == NB
MIN_NORM = 1e-15
MAX_NORM = 1.0 - 0.004
ARTANH_MAX = 1.0 - 1e-7
LN_EPS = 1e-5
PASSES = 8


def build(nc, a, out):
    ctx = ExitStack()
    with ctx:
        def sb(name, shape, dt=FP32):
            return ctx.enter_context(nc.sbuf_tensor(name, shape, dt))

        def sem(name):
            return ctx.enter_context(nc.semaphore(name))

        payload = [nc.dram_tensor(f"payload_{k}", (TILES * P, 4), I32, kind="Internal").ap() for k in ("src", "dst")]
        block_rows = [nc.dram_tensor(f"block_rows_{k}", (2, TILES), I16, kind="Internal").ap() for k in ("src", "dst")]
        table_hyp = nc.dram_tensor("table_hyp", (NB * P, TW), FP32, kind="Internal").ap()
        table_lin = nc.dram_tensor("table_lin", (NB * P, D), FP32, kind="Internal").ap()

        xs = sb("xs", [P, NB, D])
        acc = sb("acc", [P, NB, W])
        tab = sb("tab", [P, NB, TW])
        rows = sb("rows", [P, 2, G, TW])
        onehot = sb("onehot", [P, 2, G, P])
        head = sb("head", [P, G, TW])
        rel = sb("rel", [P, G, RW])
        msg = sb("msg", [P, G, W])
        type_hot = sb("type_hot", [P, G, R])
        sel_t = sb("sel_t", [P, 2, 4 * P])
        type_t = sb("type_t", [P, 2, P])
        pay = sb("pay", [P, 2, G, 4], I32)
        sc = sb("sc", [P, 34, G])
        rowoff = sb("rowoff", [1, 2, TILES], I16)
        degree = sb("degree", [P, NB, 2])
        stat = sb("stat", [P, 6, NB])
        iota = sb("iota", [P, P])
        ident = sb("ident", [P, P])
        iota_bf = sb("iota_bf", [P, NB], BF16)
        before = sb("before", [P, P], BF16)
        notbefore = sb("notbefore", [P, P], BF16)
        ones_bf = sb("ones_bf", [P, P], BF16)
        relT = sb("relT", [D, R])
        relblk = sb("relblk", [P, 4, RW])
        w_msg = sb("w_msg", [P, 2, D])
        w_cnt = sb("w_cnt", [D + 3, 2, D])
        w_ih = sb("w_ih", [D + 1, 2, 3 * D])
        w_hh = sb("w_hh", [D + 1, 2, 3 * D])
        w_c1 = sb("w_c1", [P, 2, P])
        w_c2 = sb("w_c2", [P, 2, P])
        b_c1 = sb("b_c1", [P, 2])
        b_c2 = sb("b_c2", [P, 2, D])

        flat_rows = rows[:, :, :, :].rearrange("p a b c -> p (a b c)")
        big = flat_rows[:, 0:NB * D].rearrange("p (b d) -> p b d", d=D)
        y = tab[:, :, :].rearrange("p a b -> p (a b)")[:, 0:NB * D].rearrange("p (b d) -> p b d", d=D)
        flat_hot = onehot[:, :, :, :].rearrange("p a b c -> p (a b c)")
        hist = flat_hot.bitcast(BF16)[0:EP, 0:2 * HC * NB].rearrange("p (h c b) -> p h c b", h=2, b=NB)
        flat_tab = tab[:, :, :].rearrange("p a b -> p (a b)")
        edges_in = flat_tab.bitcast(I32)[0:EP, 0:4 * EC].rearrange("p (k c) -> p k c", k=4)
        stage = flat_rows.bitcast(I32)[0:EP, 0:2 * HC * 4].rearrange("p (h c k) -> p h c k", h=2, k=4)
        keyf = flat_rows[0:EP, 400:400 + EC]
        addr = flat_rows.bitcast(I32)[0:EP, 2100:2100 + 2 * HC].rearrange("p (h c) -> p h c", h=2)
        posf = flat_rows[0:EP, 2200:2200 + HC]
        posi = flat_rows.bitcast(I32)[0:EP, 2250:2250 + 4 * HC].rearrange("p (k c) -> p k c", k=4)
        picked = flat_rows[0:EP, 2500:2500 + CH * NB].rearrange("p (c b) -> p c b", b=NB)
        start_f = flat_rows[:, 3000:3000 + CH * NB].rearrange("p (c b) -> p c b", b=NB)
        count_f = flat_rows[:, 3500:3500 + CH * NB].rearrange("p (c b) -> p c b", b=NB)
        bucket = flat_rows[:, 4000:4000 + 6 * NB].rearrange("p (k b) -> p k b", b=NB)
        bucket_i = flat_rows.bitcast(I32)[:, 4600:4600 + 2 * NB].rearrange("p (k b) -> p k b", b=NB)
        TPP = TILES // P
        tile_no = flat_rows[:, 4800:4800 + TPP]
        tile_blk = flat_rows[:, 4820:4820 + TPP]
        tile_off = flat_rows.bitcast(I16)[:, 2 * 4840:2 * 4840 + 2 * TPP].rearrange("p (k t) -> p k t", k=2)
        tile_cmp = flat_rows[:, 4900:4900 + TPP * NB].rearrange("p (t b) -> p t b", b=NB)
        fill = msg[:, :, :].rearrange("p a b -> p (a b)").bitcast(I32)[:, 0:G * 4].rearrange("p (t k) -> p t k", k=4)

        hot = flat_hot
        st_u = hot[:, 0:KB * P].rearrange("p (b c) -> p b c", c=P)
        st_x = hot[:, 1000:1000 + KB * (D + 3)].rearrange("p (b c) -> p b c", c=D + 3)
        st_uT = hot[:, 1500:1500 + KB * P].rearrange("p (b c) -> p b c", c=P)
        st_xT = hot[:, 2500:2500 + KB * P].rearrange("p (b c) -> p b c", c=P)
        st_hT = hot[:, 3500:3500 + KB * P].rearrange("p (b c) -> p b c", c=P)
        st_g = hot[:, 4500:4500 + KB * 256].rearrange("p (b c) -> p b c", c=256)
        st_o = hot[:, 6400:6400 + KB * D].rearrange("p (b c) -> p b c", c=D)

        bank = [ctx.enter_context(nc.psum_tensor(f"bank{i}", [P, 512], FP32)) for i in range(8)]
        ps_sel, ps_rel, ps_head, ps_sum = bank[0:2], bank[2:4], bank[4:6], bank[6:8]
        ps_all = bank

        tick = {k: sem(f"tick_{k}") for k in ("sp", "pool", "dve", "act", "pe")}
        arrived = sem("arrived")
        loads = sem("loads")
        stores = sem("stores")
        filled = sem("filled")
        weights_cleared = sem("weights_cleared")
        S = {}
        for k in range(2):
            for n in ("hist_ready", "hist_counted", "start_ready", "ranked", "rank_read", "staged", "hot_ready"):
                S[n, k] = sem(f"{n}_{k}")
            S["sent", k] = [sem(f"sent_{k}_{h}") for h in range(2)]
            for n in ("norms_asked", "norms_done", "q_staged", "q_transposed", "q_copied", "q_made", "q_kept"):
                S[n, k] = sem(f"{n}_{k}")
        for n in range(PASSES):
            S["loaded", n] = [sem(f"loaded_{n}_{h}") for h in range(2)]
            S["gathered", n] = [sem(f"gathered_{n}_{h}") for h in range(2)]
            for m in ("hot_made", "rows_free", "accumulated", "scattered"):
                S[m, n] = sem(f"{m}_{n}")
            if n < 2:
                for m in ("transposed", "sel_copied", "fetched", "fetch_copied", "asked", "answered"):
                    S[m, n] = sem(f"{m}_{n}")
        for n in range(4):
            for m in ("blk_staged", "blk_transposed", "blk_copied", "blk_mid", "blk_mid_kept", "blk_made", "blk_act", "blk_act2", "blk_back"):
                S[m, n + 10] = sem(f"{m}_{n}")

        block = ctx.enter_context(nc.Block())
        EPB = 5

        def meet(eng, k):
            eng.drain().then_inc(arrived, 1)
            eng.wait_ge(arrived, EPB * k)

        def await_reg(eng, who, s, v):
            eng.wait_ge(s, v)
            eng.sem_inc(tick[who], 1)

        pv = [p.rearrange("(g q t) k -> g q t k", q=P, t=G) for p in payload]

        B_CONST, B_G = 1, [2, 3]
        b_next = 4
        BN = {}
        for name in ("x", "prep0", "pass0", "hop0", "pass1", "hop1", "tab2", "pass2", "gru0", "pass3", "gru1",
                     "pass4", "c0a", "pass5", "c0b", "pass6", "c1a", "pass7", "c1b"):
            BN[name] = b_next
            b_next += 1

        @block.sync
        def _(sp):
            n = 0
            for k, name in enumerate(("src", "dst", "edge_type_33")):
                sp.dma_start(edges_in[:, k, :], a[name]).then_inc(loads, 16)
                n += 1
            sp.dma_start(edges_in[:, 3, :].bitcast(FP32), a["edge_weight1"]).then_inc(loads, 16)
            for t, name in ((iota, "iota"), (ident, "ident")):
                sp.dma_start(t[:, :], a[name]).then_inc(loads, 16)
            sp.dma_start(relT[:, :], a["relT"]).then_inc(loads, 16)
            sp.dma_start(b_c2[:, 0, :], a["L2_gnn_b2"].partition_broadcast(P)).then_inc(loads, 16)
            sp.dma_start(b_c2[:, 1, :], a["L3_gnn_b2"].partition_broadcast(P)).then_inc(loads, 16)
            n += 6
            sp.wait_ge(weights_cleared, 1)
            for j in range(4):
                sp.dma_start(relblk[R * j:R * j + R, j, 0:D], a["L0_gnn_relation_emb"]).then_inc(loads, 16)
                n += 1
            for t in range(2):
                sp.dma_start(w_msg[:, t, :], a["msg_WT"][t, 0:2 * D, :]).then_inc(loads, 16)
                sp.dma_start(w_cnt[D + 1:D + 2, t, :], a["L1_gnn_msg_b"][t:t + 1, :]).then_inc(loads, 16)
                sp.dma_start(w_cnt[D + 2:D + 3, t, :], a["msg_WT"][t, 2 * D:2 * D + 1, :]).then_inc(loads, 16)
                sp.dma_start(w_ih[0:D, t, :], a["WihT"][t]).then_inc(loads, 16)
                sp.dma_start(w_ih[D:D + 1, t, :], a["L1_gnn_gru_bih"][t:t + 1, :]).then_inc(loads, 16)
                sp.dma_start(w_hh[0:D, t, :], a["WhhT"][t]).then_inc(loads, 16)
                sp.dma_start(w_hh[D:D + 1, t, :], a["L1_gnn_gru_bhh"][t:t + 1, :]).then_inc(loads, 16)
                n += 7
            for l, (h, names) in enumerate(((16, ("L2_gnn_W1_l", "L2_gnn_W1_r", "L2_gnn_W2_l", "L2_gnn_W2_r", "L2_b1c")),
                                            (128, ("L3_W1_lT", "L3_W1_rT", "L3_W2_lT", "L3_W2_rT", "L3_b1c")))):
                sp.dma_start(w_c1[0:D, l, 0:h], a[names[0]]).then_inc(loads, 16)
                sp.dma_start(w_c1[D:P, l, 0:h], a[names[1]]).then_inc(loads, 16)
                sp.dma_start(w_c2[0:h, l, 0:D], a[names[2]]).then_inc(loads, 16)
                sp.dma_start(w_c2[0:h, l, D:P], a[names[3]]).then_inc(loads, 16)
                sp.dma_start(b_c1[0:h, l:l + 1], a[names[4]]).then_inc(loads, 16)
                n += 5
            sp.dma_start(xs[:, 0:NB - 1, :], a["x"][0:(NB - 1) * P, :].rearrange("(b p) d -> p b d", p=P)).then_inc(loads, 16)
            sp.dma_start(xs[0:LAST, NB - 1, :], a["x"][(NB - 1) * P:N, :]).then_inc(loads, 16)
            n += 2
            sp.wait_ge(filled, 1)
            with sp.Fori(0, GROUPS) as g:
                for k in range(2):
                    sp.dma_start(pv[k][bass.ds(g, 1)].rearrange("a q t k -> (a q) t k"), fill).then_inc(stores, 16)
            sp.wait_ge(stores, 2 * GROUPS * 16)
            sp.wait_ge(loads, n * 16)
            meet(sp, B_CONST)
            stored = 2 * GROUPS * 16
            for k in range(2):
                sp.wait_ge(S["start_ready", k], 1)
                sp.dma_start(block_rows[k].rearrange("k (p t) -> p k t", p=P), tile_off).then_inc(stores, 16)
                stored += 16
                sp.wait_ge(stores, stored)
                meet(sp, B_G[k])
            meet(sp, BN["x"])

            def load_rowoff(k):
                nonlocal n
                sp.dma_start(rowoff[0:1, :, :].rearrange("p k t -> p (k t)"),
                             block_rows[k].rearrange("k t -> (k t)").unsqueeze(0)).then_inc(loads, 16)
                n += 1
                sp.wait_ge(loads, n * 16)

            def run_pass(m, k):
                with sp.Fori(0, ITERS) as i:
                    for h in range(2):
                        await_reg(sp, "sp", S["rows_free", m], 2 * i + (h + 1))
                        sp.dma_start(pay[:, h, :, :],
                                     pv[k][bass.ds(2 * i + h, 1)].rearrange("a q t k -> (a q) t k")).then_inc(S["loaded", m][h], 16)
                sp.wait_ge(S["loaded", m][1], ITERS * 16)
                sp.wait_ge(S["loaded", m][0], ITERS * 16)
                meet(sp, BN[f"pass{m}"])

            def store_table(dst, srcv):
                nonlocal stored
                sp.dma_start(dst.rearrange("(b p) c -> p b c", p=P), srcv).then_inc(stores, 16)
                stored += 16
                sp.wait_ge(stores, stored)

            load_rowoff(0)
            sp.wait_ge(S["q_kept", 0], NITERS)
            store_table(table_hyp, tab[:, :, :])
            meet(sp, BN["prep0"])
            run_pass(0, 0)
            sp.wait_ge(S["q_kept", 1], NITERS)
            store_table(table_hyp, tab[:, :, :])
            meet(sp, BN["hop0"])
            run_pass(1, 0)
            meet(sp, BN["hop1"])
            store_table(table_lin, xs[:, :, :])
            meet(sp, BN["tab2"])
            run_pass(2, 0)
            sp.wait_ge(S["blk_back", 10], NITERS)
            store_table(table_lin, y)
            meet(sp, BN["gru0"])
            run_pass(3, 0)
            sp.wait_ge(S["blk_back", 11], NITERS + 1)
            store_table(table_lin, xs[:, :, :])
            load_rowoff(1)
            meet(sp, BN["gru1"])
            for l in range(2):
                run_pass(4 + 2 * l, 1)
                sp.wait_ge(S["blk_back", 12 + l], NITERS)
                store_table(table_lin, big)
                meet(sp, BN[f"c{l}a"])
                run_pass(5 + 2 * l, 1)
                if l == 0:
                    sp.wait_ge(S["blk_back", 12], NITERS + 1)
                    store_table(table_lin, xs[:, :, :])
                    meet(sp, BN["c0b"])
                else:
                    sp.wait_ge(S["blk_back", 13], NITERS + 1)
                    sp.dma_start(out[0:(NB - 1) * P, :].rearrange("(b p) d -> p b d", p=P), xs[:, 0:NB - 1, :]).then_inc(stores, 16)
                    sp.dma_start(out[(NB - 1) * P:N, :], xs[0:LAST, NB - 1, :]).then_inc(stores, 16)
                    stored += 32
                    sp.wait_ge(stores, stored)
                    meet(sp, BN["c1b"])

        @block.gpsimd
        def _(pool):
            meet(pool, B_CONST)
            for k in range(2):
                sent = S["sent", k]
                with pool.Fori(0, GITERS) as i:
                    for h in range(2):
                        await_reg(pool, "pool", S["staged", k], 2 * i + (h + 1))
                        for c in range(HC):
                            pool.indirect_dma_start(
                                out=payload[k][:, :], out_offset=bass.IndirectOffsetOnAxis(ap=addr[:, h, c:c + 1], axis=0),
                                in_=stage[:, h, c, :], in_offset=None).then_inc(sent[h], 16)
                for h in range(2):
                    pool.wait_ge(sent[h], GITERS * HC * 16)
                meet(pool, B_G[k])
            meet(pool, BN["x"])
            meet(pool, BN["prep0"])

            def run_pass(m):
                table, width = (table_hyp, TW) if m < 2 else (table_lin, D)
                with pool.Fori(0, ITERS) as i:
                    for h in range(2):
                        await_reg(pool, "pool", S["loaded", m][h], 16 * i + 16)
                        await_reg(pool, "pool", S["rows_free", m], 2 * i + (h + 1))
                        for t in range(G):
                            pool.indirect_dma_start(
                                out=rows[:, h, t, 0:width], out_offset=None, in_=table[:, :],
                                in_offset=bass.IndirectOffsetOnAxis(ap=pay[:, h, t, 0:1], axis=0)).then_inc(S["gathered", m][h], 16)
                for h in range(2):
                    pool.wait_ge(S["gathered", m][h], ITERS * G * 16)
                meet(pool, BN[f"pass{m}"])

            run_pass(0)
            meet(pool, BN["hop0"])
            run_pass(1)
            meet(pool, BN["hop1"])
            meet(pool, BN["tab2"])
            run_pass(2)
            meet(pool, BN["gru0"])
            run_pass(3)
            meet(pool, BN["gru1"])
            for l in range(2):
                run_pass(4 + 2 * l)
                meet(pool, BN[f"c{l}a"])
                run_pass(5 + 2 * l)
                meet(pool, BN[f"c{l}b"])

        @block.tensor
        def _(pe):
            meet(pe, B_CONST)
            for k in range(2):
                totals = bank[0]
                pe.wait_ge(S["hot_ready", k], 1)
                nc.tensor.matmul(totals[:, 0:CH * NB], ones_bf[0:EP, :], hist[:, 0, 0:CH, :].rearrange("p c b -> p (c b)"),
                                 start=True, stop=False, skip_group_check=True)
                for c in range(1, NCH):
                    last = nc.tensor.matmul(totals[:, 0:CH * NB], ones_bf[0:EP, :],
                                            hist[:, 0, c * CH:c * CH + CH, :].rearrange("p c b -> p (c b)"),
                                            start=False, stop=False, skip_group_check=True)
                last.then_inc(S["hist_counted", k], 1)
                with pe.Fori(0, 2 * GITERS - 1) as i:
                    await_reg(pe, "pe", S["hot_ready", k], i + 2)
                    for c in range(NCH):
                        last = nc.tensor.matmul(totals[:, 0:CH * NB], ones_bf[0:EP, :],
                                                hist[:, 0, c * CH:c * CH + CH, :].rearrange("p c b -> p (c b)"),
                                                start=False, stop=False, skip_group_check=True)
                    last.then_inc(S["hist_counted", k], 1)
                place = bank[1]
                pe.wait_ge(S["start_ready", k], 1)
                nc.tensor.matmul(place[0:EP, 0:CH * NB], ident[:, 0:EP], start_f.rearrange("p c b -> p (c b)"),
                                 start=True, stop=False, skip_group_check=True)
                with pe.Fori(0, GITERS) as i:
                    for h in range(2):
                        await_reg(pe, "pe", S["hist_ready", k], 2 * i + (h + 1))
                        for c in range(NCH):
                            hot_c = hist[:, h, c * CH:c * CH + CH, :].rearrange("p c b -> p (c b)")
                            nc.tensor.matmul(place[0:EP, 0:CH * NB], before[0:EP, 0:EP], hot_c,
                                             start=False, stop=False, skip_group_check=True).then_inc(S["ranked", k], 1)
                            await_reg(pe, "pe", S["rank_read", k], (2 * i + h) * NCH + (c + 1))
                            nc.tensor.matmul(place[0:EP, 0:CH * NB], notbefore[0:EP, 0:EP], hot_c,
                                             start=False, stop=False, skip_group_check=True)
                meet(pe, B_G[k])
            meet(pe, BN["x"])

            def make_q(k):
                with pe.Fori(0, NITERS) as i:
                    await_reg(pe, "pe", S["q_staged", k], i + 1)
                    for j in range(KB):
                        last = nc.tensor.transpose(bank[j // 4][0:D, (j % 4) * P:(j % 4) * P + P], st_u[:, j, 0:D], ident[:, :])
                    last.then_inc(S["q_transposed", k], 1)
                    await_reg(pe, "pe", S["q_copied", k], i + 1)
                    for j in range(KB):
                        last = nc.tensor.matmul(bank[2][:, j * R:j * R + R], st_uT[0:D, j, :], relT[:, :], start=True, stop=True)
                    last.then_inc(S["q_made", k], 1)

            regs = [pe.alloc_register(f"head_block_{j}") for j in range(4)]

            def run_pass(m):
                hyp = m < 2
                with pe.Fori(0, ITERS) as i:
                    for h in range(2):
                        await_reg(pe, "pe", S["hot_made", m], 2 * i + (h + 1))
                        if hyp:
                            def turn(q):
                                await_reg(pe, "pe", S["fetch_copied", m], (2 * i + h) * QG + (q + 1))
                                for j in range(4):
                                    nc.tensor.transpose(ps_sel[q % 2][:, j * P:j * P + P], onehot[:, h, 4 * q + j, :], ident[:, :])
                                nc.tensor.transpose(ps_rel[q % 2][:, 0:P], type_hot[:, 4 * q:4 * q + 4, :].rearrange("p a b -> p (a b)"),
                                                    ident[:, :]).then_inc(S["transposed", m], 1)

                            def fetch(q):
                                pe.load(regs, rowoff[0:1, 1, bass.ds((2 * i + h) * G + 4 * q, 4)])
                                await_reg(pe, "pe", S["sel_copied", m], (2 * i + h) * QG + (q + 1))
                                for j in range(4):
                                    b = pe.snap(regs[j], min_val=0, max_val=(NB - 1) * TW)
                                    nc.tensor.matmul(ps_head[q % 2][:, j * TW:j * TW + TW], sel_t[:, q % 2, j * P:j * P + P],
                                                     flat_tab[:, bass.ds(b, TW)], start=True, stop=True)
                                nc.tensor.matmul(ps_rel[q % 2][:, P:P + 4 * RW], type_t[:, q % 2, :],
                                                 relblk[:, :, :].rearrange("p a b -> p (a b)"),
                                                 start=True, stop=True).then_inc(S["fetched", m], 1)
                            turn(0)
                            for q in range(1, QG):
                                turn(q)
                                fetch(q - 1)
                            fetch(QG - 1)
                            await_reg(pe, "pe", S["answered", m], 5 * (2 * i + h) + 5)
                        else:
                            await_reg(pe, "pe", S["gathered", m][h], (i + 1) * (G * 16))
                        for q in range(QG):
                            await_reg(pe, "pe", S["accumulated", m], (2 * i + h) * QG + (q + 1))
                            for j in range(4):
                                t = 4 * q + j
                                mv = msg[:, t, 0:W] if hyp else rows[:, h, t, 0:W]
                                last = nc.tensor.matmul(ps_sum[q % 2][:, j * W:j * W + W], onehot[:, h, t, :], mv, start=True, stop=True)
                            last.then_inc(S["scattered", m], 1)
                meet(pe, BN[f"pass{m}"])

            def gru(t):
                s = 10 + t
                with pe.Fori(0, NITERS) as i:
                    await_reg(pe, "pe", S["blk_staged", s], i + 1)
                    for j in range(KB):
                        nc.tensor.transpose(bank[j // 4][:, (j % 4) * P:(j % 4) * P + P], st_u[:, j, :], ident[:, :])
                    for j in range(KB):
                        last = nc.tensor.transpose(bank[2 + j // 4][0:D + 3, (j % 4) * P:(j % 4) * P + P], st_x[:, j, :], ident[:, :])
                    last.then_inc(S["blk_transposed", s], 1)
                    await_reg(pe, "pe", S["blk_copied", s], i + 1)
                    for j in range(KB):
                        o = bank[4 + j // 4][0:D, (j % 4) * P:(j % 4) * P + P]
                        nc.tensor.matmul(o, w_msg[:, t, :], st_uT[:, j, :], start=True, stop=False)
                        last = nc.tensor.matmul(o, w_cnt[:, t, :], st_xT[0:D + 3, j, :], start=False, stop=True)
                    last.then_inc(S["blk_mid", s], 1)
                    await_reg(pe, "pe", S["blk_mid_kept", s], i + 1)
                    for j in range(KB):
                        bk, o = bank[j // 2], (j % 2) * 256
                        nc.tensor.matmul(bk[:, o:o + P], st_hT[0:D + 1, j, :], w_ih[:, t, 0:P], start=True, stop=False)
                        nc.tensor.matmul(bk[:, o:o + P], st_xT[0:D + 1, j, :], w_hh[:, t, 0:P], start=False, stop=True)
                        nc.tensor.matmul(bk[:, o + P:o + P + D], st_hT[0:D + 1, j, :], w_ih[:, t, P:3 * D], start=True, stop=True)
                        last = nc.tensor.matmul(bk[:, o + P + D:o + 256], st_xT[0:D + 1, j, :], w_hh[:, t, P:3 * D], start=True, stop=True)
                    last.then_inc(S["blk_made", s], 1)

            def conv(l):
                s = 12 + l
                with pe.Fori(0, NITERS) as i:
                    await_reg(pe, "pe", S["blk_staged", s], i + 1)
                    for j in range(KB):
                        last = nc.tensor.transpose(bank[j // 4][:, (j % 4) * P:(j % 4) * P + P], st_u[:, j, :], ident[:, :])
                    last.then_inc(S["blk_transposed", s], 1)
                    await_reg(pe, "pe", S["blk_copied", s], i + 1)
                    for j in range(KB):
                        last = nc.tensor.matmul(bank[2 + j // 4][:, (j % 4) * P:(j % 4) * P + P], w_c1[:, l, :], st_uT[:, j, :],
                                                start=True, stop=True)
                    last.then_inc(S["blk_mid", s], 1)
                    await_reg(pe, "pe", S["blk_mid_kept", s], i + 1)
                    for j in range(KB):
                        last = nc.tensor.matmul(bank[4 + j // 4][:, (j % 4) * P:(j % 4) * P + P], st_hT[:, j, :], w_c2[:, l, :],
                                                start=True, stop=True)
                    last.then_inc(S["blk_made", s], 1)

            make_q(0)
            meet(pe, BN["prep0"])
            run_pass(0)
            make_q(1)
            meet(pe, BN["hop0"])
            run_pass(1)
            meet(pe, BN["hop1"])
            meet(pe, BN["tab2"])
            run_pass(2)
            gru(0)
            meet(pe, BN["gru0"])
            run_pass(3)
            gru(1)
            meet(pe, BN["gru1"])
            for l in range(2):
                run_pass(4 + 2 * l)
                conv(l)
                meet(pe, BN[f"c{l}a"])
                run_pass(5 + 2 * l)
                meet(pe, BN[f"c{l}b"])

        names = iter(range(34))

        def s1():
            return sc[:, next(names), :]

        def s2():
            q = next(names)
            next(names)
            return sc[:, q:q + 2, :]

        KC, XP = s1(), s1()
        NN, YY, HY, BN2, C1, C2, T1, T2, NR, SQ = s2(), s2(), s2(), s2(), s2(), s2(), s2(), s2(), s2(), s2()
        TR, XY, MM, DD, DC, E1, E2, E3, U1, U2, U3, OM = (s1() for _ in range(12))

        @block.scalar
        def _(act):
            meet(act, B_CONST)
            for k in range(2):
                meet(act, B_G[k])
            meet(act, BN["x"])

            def norms(k):
                act.wait_ge(S["norms_asked", k], 1)
                if k == 0:
                    nc.scalar.activation(relblk[:, :, D + 1], relblk[:, :, D], ACT.Sqrt)
                nc.scalar.activation(stat[:, 1, :], stat[:, 0, :], ACT.Sqrt).then_inc(S["norms_done", k], 1)
                act.wait_ge(S["norms_asked", k], 2)
                nc.scalar.activation(stat[:, 2, :], stat[:, 1, :], ACT.Tanh).then_inc(S["norms_done", k], 1)

            def make_q(k):
                with act.Fori(0, NITERS) as i:
                    await_reg(act, "act", S["q_transposed", k], i + 1)
                    nc.scalar.copy(st_uT[0:D, 0:4, :], bank[0][0:D, :].rearrange("p (b c) -> p b c", c=P))
                    nc.scalar.copy(st_uT[0:D, 4:KB, :], bank[1][0:D, 0:(KB - 4) * P].rearrange("p (b c) -> p b c", c=P)
                                   ).then_inc(S["q_copied", k], 1)

            def run_pass(m):
                if m >= 2:
                    meet(act, BN[f"pass{m}"])
                    return
                act.sem_inc(S["fetch_copied", m], 2)
                with act.Fori(0, ITERS) as i:
                    for h in range(2):
                        def copy_sel(q):
                            await_reg(act, "act", S["transposed", m], (2 * i + h) * QG + (q + 1))
                            nc.scalar.copy(sel_t[:, q % 2, :], ps_sel[q % 2][:, :])
                            nc.scalar.copy(type_t[:, q % 2, :], ps_rel[q % 2][:, 0:P]).then_inc(S["sel_copied", m], 1)

                        def copy_fetch(q):
                            await_reg(act, "act", S["fetched", m], (2 * i + h) * QG + (q + 1))
                            nc.scalar.copy(head[:, 4 * q:4 * q + 4, :].rearrange("p a b -> p (a b)"), ps_head[q % 2][:, 0:4 * TW])
                            nc.scalar.copy(rel[:, 4 * q:4 * q + 4, :].rearrange("p a b -> p (a b)"),
                                           ps_rel[q % 2][:, P:P + 4 * RW]).then_inc(S["fetch_copied", m], 1)
                        copy_sel(0)
                        for q in range(1, QG):
                            copy_sel(q)
                            copy_fetch(q - 1)
                        copy_fetch(QG - 1)
                        for n, (o, iv, f) in enumerate(((T1, T1, ACT.Tanh), (U1, U1, ACT.Sqrt), (SQ, SQ, ACT.Sqrt), (U1, U1, ACT.Ln))):
                            await_reg(act, "act", S["asked", m], 5 * (2 * i + h) + (n + 1))
                            nc.scalar.activation(o, iv, f).then_inc(S["answered", m], 1)
                        await_reg(act, "act", S["asked", m], 5 * (2 * i + h) + 5)
                        nc.scalar.activation(msg[:, :, 0:D], head[:, :, 0:D], ACT.Relu).then_inc(S["answered", m], 1)
                meet(act, BN[f"pass{m}"])

            def root(k, c):
                act.wait_ge(S["norms_asked", k], c)
                nc.scalar.activation(stat[:, 1, :], stat[:, 0, :], ACT.Sqrt).then_inc(S["norms_done", k], 1)

            norms(0)
            make_q(0)
            meet(act, BN["prep0"])
            run_pass(0)
            root(0, 3)
            norms(1)
            make_q(1)
            meet(act, BN["hop0"])
            run_pass(1)
            root(1, 3)
            root(1, 4)
            meet(act, BN["hop1"])
            meet(act, BN["tab2"])

            def copy_turned(s, both):
                nc.scalar.copy(st_uT[:, 0:4, :], bank[0][:, :].rearrange("p (b c) -> p b c", c=P))
                last = nc.scalar.copy(st_uT[:, 4:KB, :], bank[1][:, 0:(KB - 4) * P].rearrange("p (b c) -> p b c", c=P))
                if both:
                    nc.scalar.copy(st_xT[0:D + 3, 0:4, :], bank[2][0:D + 3, :].rearrange("p (b c) -> p b c", c=P))
                    last = nc.scalar.copy(st_xT[0:D + 3, 4:KB, :], bank[3][0:D + 3, 0:(KB - 4) * P].rearrange("p (b c) -> p b c", c=P))
                last.then_inc(S["blk_copied", s], 1)

            def gru(t):
                s = 10 + t
                with act.Fori(0, NITERS) as i:
                    await_reg(act, "act", S["blk_transposed", s], i + 1)
                    copy_turned(s, True)
                    await_reg(act, "act", S["blk_mid", s], i + 1)
                    nc.scalar.copy(st_hT[0:D, 0:4, :], bank[4][0:D, :].rearrange("p (b c) -> p b c", c=P))
                    nc.scalar.copy(st_hT[0:D, 4:KB, :], bank[5][0:D, 0:(KB - 4) * P].rearrange("p (b c) -> p b c", c=P)
                                   ).then_inc(S["blk_mid_kept", s], 1)
                    await_reg(act, "act", S["blk_made", s], i + 1)
                    for b in range(4):
                        w = min(2, KB - 2 * b)
                        v = bank[b][:, 0:w * 256].rearrange("p (b c) -> p b c", c=256)
                        nc.scalar.activation(st_g[:, 2 * b:2 * b + w, 0:P], v[:, :, 0:P], ACT.Sigmoid)
                        last = nc.scalar.copy(st_g[:, 2 * b:2 * b + w, P:256], v[:, :, P:256])
                    last.then_inc(S["blk_act", s], 1)
                    await_reg(act, "act", S["blk_act2", s], i + 1)
                    nc.scalar.activation(st_o[:, :, :], st_g[:, :, P:P + D], ACT.Tanh).then_inc(S["blk_act", s], 1)
                if t == 1:
                    act.wait_ge(S["blk_act2", s], NITERS + 1)
                    nc.scalar.activation(stat[:, 1, :], stat[:, 0, :], ACT.Sqrt).then_inc(S["blk_act", s], 1)

            def conv(l):
                s = 12 + l
                with act.Fori(0, NITERS) as i:
                    await_reg(act, "act", S["blk_transposed", s], i + 1)
                    copy_turned(s, False)
                    await_reg(act, "act", S["blk_mid", s], i + 1)
                    nc.scalar.activation(st_hT[:, 0:4, :], bank[2][:, :].rearrange("p (b c) -> p b c", c=P), ACT.Relu, bias=b_c1[:, l:l + 1])
                    nc.scalar.activation(st_hT[:, 4:KB, :], bank[3][:, 0:(KB - 4) * P].rearrange("p (b c) -> p b c", c=P), ACT.Relu,
                                         bias=b_c1[:, l:l + 1]).then_inc(S["blk_mid_kept", s], 1)

            run_pass(2)
            gru(0)
            meet(act, BN["gru0"])
            run_pass(3)
            gru(1)
            meet(act, BN["gru1"])
            for l in range(2):
                run_pass(4 + 2 * l)
                conv(l)
                meet(act, BN[f"c{l}a"])
                run_pass(5 + 2 * l)
                act.wait_ge(S["blk_act2", 12 + l], 1)
                nc.scalar.activation(stat[:, 1, :], stat[:, 0, :], ACT.Sqrt).then_inc(S["blk_act", 12 + l], 1)
                meet(act, BN[f"c{l}b"])

        @block.vector
        def _(dve):
            V = nc.vector

            def tt(o, x, y_, op, last=True):
                r = V.tensor_tensor(o, x, y_, op)
                if last:
                    dve.drain()
                return r

            def ts(o, x, c1, op1, c2=None, op2=None):
                if op2 is None:
                    V.tensor_scalar(o, x, c1, None, op1)
                else:
                    V.tensor_scalar(o, x, c1, c2, op1, op2)
                dve.drain()

            def stt(o, x, c, y_, o1, o2):
                V.scalar_tensor_tensor(out=o, in0=x, scalar=c, in1=y_, op0=o1, op1=o2)
                dve.drain()

            def recip(o, x):
                V.reciprocal(o, x)
                dve.drain()

            def rsum(o, x):
                V.reduce_sum(o, x, axis=AX.X)
                dve.drain()

            def over(v, w):
                return v.unsqueeze(2).to_broadcast([v.shape[0], v.shape[1], w])

            for t in (relblk, w_cnt, w_c1, w_c2, b_c1):
                V.memset(t[:], 0.0)
            V.memset(xs[64:128, NB - 1, :], 0.0)
            dve.drain().then_inc(weights_cleared, 1)
            V.memset(fill[:, :, 0:1], 0)
            V.memset(fill[:, :, 1:2], -1)
            V.memset(fill[:, :, 2:3], 1)
            V.memset(fill[:, :, 3:4], 0)
            dve.drain().then_inc(filled, 1)
            V.memset(ones_bf[:, :], 1.0)
            dve.drain()
            meet(dve, B_CONST)
            V.tensor_copy(iota_bf[:, :], iota[:, 0:NB])
            tt(start_f.rearrange("p c b -> p (c b)")[:, 0:P], ident[:, :], iota[:, :], ALU.mult)
            rsum(stat[:, 0, 0:1], start_f.rearrange("p c b -> p (c b)")[:, 0:P])
            V.tensor_scalar(before[:, :], iota[:, :], stat[:, 0, 0:1], None, ALU.is_gt)
            V.tensor_scalar(notbefore[:, :], iota[:, :], stat[:, 0, 0:1], None, ALU.is_le)
            V.tensor_scalar(bucket[:, 0, 0:1], stat[:, 0, 0:1], float(TPP), None, ALU.mult)
            TY = keyf
            V.tensor_copy(TY, edges_in[:, 2, :])
            dve.drain()
            V.tensor_scalar(tile_no, iota[:, 0:TPP], bucket[:, 0, 0:1], None, ALU.add)
            ty0 = hist[:, 0, :, :].rearrange("p c b -> p (c b)")[:, 0:EC]
            ts(ty0, TY, 0.0, ALU.is_equal)
            stt(TY, ty0, float(R), TY, ALU.mult, ALU.add)
            V.tensor_copy(edges_in[:, 2, :], TY)
            V.tensor_copy(stat[:, 5, 0:TPP], tile_no)
            dve.drain()

            def make_hist(h, c0):
                V.tensor_tensor(hist[:, h, :, :], over(keyf[:, bass.ds(c0, HC)], NB),
                                iota_bf[0:EP, :].unsqueeze(1).to_broadcast([EP, HC, NB]), ALU.is_equal)

            for k in range(2):
                key = edges_in[:, k, :]
                tmpi = flat_rows.bitcast(I32)[0:EP, 2500:2500 + EC]
                V.tensor_scalar(tmpi, key, 7, None, ALU.arith_shift_right)
                dve.drain()
                V.tensor_copy(keyf, tmpi)
                dve.drain()
                V.tensor_tensor(hist[:, 0, :, :], over(keyf[:, 0:HC], NB), iota_bf[0:EP, :].unsqueeze(1).to_broadcast([EP, HC, NB]),
                                ALU.is_equal).then_inc(S["hot_ready", k], 1)
                with dve.Fori(0, 2 * GITERS - 1) as i:
                    await_reg(dve, "dve", S["hist_counted", k], i + 1)
                    make_hist(0, (i + 1) * HC)
                    dve.drain().then_inc(S["hot_ready", k], 1)
                dve.wait_ge(S["hist_counted", k], 2 * GITERS)
                V.tensor_copy(count_f.rearrange("p c b -> p (c b)"), bank[0][:, 0:CH * NB])
                dve.drain()
                rsum(bucket[:, 1, :], count_f.rearrange("p c b -> p b c"))
                ts(bucket[:, 2, :], bucket[:, 1, :], float(P - 1), ALU.add)
                V.tensor_copy(bucket_i[:, 0, :], bucket[:, 2, :])
                dve.drain()
                V.tensor_scalar(bucket_i[:, 1, :], bucket_i[:, 0, :], 7, None, ALU.arith_shift_right)
                dve.drain()
                V.tensor_copy(bucket[:, 2, :], bucket_i[:, 1, :])
                V.memset(bucket[:, 3, :], 1.0)
                dve.drain()
                V.tensor_tensor_scan(bucket[:, 4, :], bucket[:, 3, :], bucket[:, 2, :], 0.0, ALU.mult, ALU.add)
                dve.drain()
                tt(bucket[:, 5, :], bucket[:, 4, :], bucket[:, 2, :], ALU.subtract)
                ts(start_f[:, 0, :], bucket[:, 5, :], float(P), ALU.mult)
                for c in range(1, CH):
                    tt(start_f[:, c, :], start_f[:, c - 1, :], count_f[:, c - 1, :], ALU.add)
                tt(tile_cmp, over(stat[:, 5, 0:TPP], NB), bucket[:, 4, :].unsqueeze(1).to_broadcast([P, TPP, NB]), ALU.is_ge)
                rsum(tile_blk, tile_cmp)
                ts(tile_blk, tile_blk, float(NB - 1), ALU.min)
                V.tensor_scalar(tile_off[:, 0, :], tile_blk, float(W), None, ALU.mult)
                V.tensor_scalar(tile_off[:, 1, :], tile_blk, float(TW), None, ALU.mult)
                dve.drain().then_inc(S["start_ready", k], 1)
                with dve.Fori(0, GITERS) as i:
                    for h in range(2):
                        c0 = i * (2 * HC) + h * HC
                        make_hist(h, c0)
                        dve.drain().then_inc(S["hist_ready", k], 1)
                        await_reg(dve, "dve", S["sent", k][h], i * (HC * 16))
                        V.tensor_copy(stage[:, h, :, 0], edges_in[:, 1 - k, bass.ds(c0, HC)])
                        V.tensor_scalar(stage[:, h, :, 1], edges_in[:, k, bass.ds(c0, HC)], P - 1, None, ALU.bitwise_and)
                        V.tensor_copy(stage[:, h, :, 2], edges_in[:, 2, bass.ds(c0, HC)])
                        V.tensor_copy(stage[:, h, :, 3].bitcast(FP32), edges_in[:, 3, bass.ds(c0, HC)].bitcast(FP32))
                        dve.drain()
                        for c in range(NCH):
                            await_reg(dve, "dve", S["ranked", k], (2 * i + h) * NCH + (c + 1))
                            V.tensor_tensor(picked, bank[1][0:EP, 0:CH * NB].rearrange("p (c b) -> p c b", b=NB),
                                            hist[:, h, c * CH:c * CH + CH, :], ALU.mult).then_inc(S["rank_read", k], 1)
                            dve.drain()
                            rsum(posf[:, c * CH:c * CH + CH], picked)
                        V.tensor_copy(posi[:, 0, :], posf)
                        dve.drain()
                        V.tensor_scalar(posi[:, 1, :], posi[:, 0, :], P - 1, 5, ALU.bitwise_and, ALU.logical_shift_left)
                        V.tensor_scalar(posi[:, 2, :], posi[:, 0, :], 7, G - 1, ALU.arith_shift_right, ALU.bitwise_and)
                        V.tensor_scalar(posi[:, 3, :], posi[:, 0, :], -(P * G), None, ALU.bitwise_and)
                        dve.drain()
                        V.tensor_tensor(posi[:, 1, :], posi[:, 1, :], posi[:, 2, :], ALU.bitwise_or)
                        dve.drain()
                        V.tensor_tensor(addr[:, h, :], posi[:, 1, :], posi[:, 3, :], ALU.bitwise_or)
                        dve.drain().then_inc(S["staged", k], 1)
                meet(dve, B_G[k])

            tt(big[:, 0:4, :], relblk[:, :, 0:D], relblk[:, :, 0:D], ALU.mult)
            rsum(relblk[:, :, D], big[:, 0:4, :])
            V.tensor_copy(tab[:, :, 0:D], xs[:, :, :])
            V.memset(msg[:, :, D:W], 1.0)
            V.memset(rows[:, :, :, D:W], 1.0)
            meet(dve, BN["x"])

            def squares(v, o):
                tt(big, v, v, ALU.mult)
                rsum(o, big)

            def prepare(k):
                squares(tab[:, :, 0:D], tab[:, :, C_EE])
                V.tensor_copy(stat[:, 0, :], tab[:, :, C_EE])
                dve.drain().then_inc(S["norms_asked", k], 1)
                dve.wait_ge(S["norms_done", k], 1)
                ts(stat[:, 1, :], stat[:, 1, :], MIN_NORM, ALU.max)
                dve.drain().then_inc(S["norms_asked", k], 1)
                dve.wait_ge(S["norms_done", k], 2)
                recip(stat[:, 3, :], stat[:, 1, :])
                tt(stat[:, 4, :], stat[:, 2, :], stat[:, 3, :], ALU.mult)
                V.tensor_copy(tab[:, :, C_NE], stat[:, 1, :])
                V.tensor_copy(tab[:, :, C_A], stat[:, 4, :])
                tt(stat[:, 3, :], stat[:, 4, :], stat[:, 4, :], ALU.mult)
                tt(tab[:, :, C_PP], stat[:, 3, :], stat[:, 0, :], ALU.mult)
                with dve.Fori(0, NITERS) as i:
                    V.tensor_copy(st_u[:, :, 0:D], tab[:, bass.ds(i * KB, KB), 0:D])
                    dve.drain().then_inc(S["q_staged", k], 1)
                    await_reg(dve, "dve", S["q_made", k], i + 1)
                    V.tensor_copy(tab[:, bass.ds(i * KB, KB), D:D + R], bank[2][:, 0:KB * R].rearrange("p (b c) -> p b c", c=R))
                    dve.drain().then_inc(S["q_kept", k], 1)

            regs = [dve.alloc_register(f"sum_block_{j}") for j in range(8)]
            flat_acc = acc[:, :, :].rearrange("p a b -> p (a b)")

            def ask(m, base, n):
                dve.drain().then_inc(S["asked", m], 1)
                await_reg(dve, "dve", S["answered", m], base + n)

            def messages(m, h, i):
                base = 5 * (2 * i + h)
                t_, q_ = rows[:, h, :, :], msg
                V.tensor_copy(NN[:, 0, :], t_[:, :, C_NE])
                V.tensor_copy(YY[:, 0, :], t_[:, :, C_EE])
                V.tensor_scalar(NN[:, 1, :], rel[:, :, D + 1], MIN_NORM, None, ALU.max)
                V.tensor_copy(YY[:, 1, :], rel[:, :, D])
                prod = msg[:, :, 0:D]
                tt(prod, head[:, :, 0:D], t_[:, :, 0:D], ALU.mult)
                rsum(HY[:, 0, :], prod)
                tt(prod[:, :, 0:R], head[:, :, D:D + R], type_hot[:, :, :], ALU.mult)
                rsum(HY[:, 1, :], prod[:, :, 0:R])
                tt(prod[:, :, 0:R], t_[:, :, D:D + R], type_hot[:, :, :], ALU.mult)
                rsum(TR, prod[:, :, 0:R])
                ss, aa, pp = head[:, :, C_EE], head[:, :, C_A], head[:, :, C_PP]

                def both(v):
                    return v.unsqueeze(1).to_broadcast([P, 2, G])
                ts(OM, pp, -1.0, ALU.mult, 1.0, ALU.add)
                ts(KC, OM, MIN_NORM, ALU.max)
                recip(XP, KC)
                tt(T1, NN, both(XP), ALU.mult)
                ask(m, base, 1)
                recip(BN2, NN)
                tt(BN2, T1, BN2, ALU.mult)
                tt(T1, BN2, BN2, ALU.mult)
                tt(T1, T1, YY, ALU.mult)
                tt(T2, BN2, HY, ALU.mult)
                tt(T2, T2, both(aa), ALU.mult)
                stt(C1, T2, 2.0, T1, ALU.mult, ALU.add)
                tt(C2, T1, both(pp), ALU.mult)
                stt(C2, T2, 2.0, C2, ALU.mult, ALU.add)
                ts(C2, C2, 1.0, ALU.add)
                ts(T2, C2, MIN_NORM, ALU.max)
                recip(T2, T2)
                tt(NR, C1, both(pp), ALU.add)
                tt(NR, NR, C2, ALU.mult)
                tt(NR, NR, T2, ALU.mult)
                tt(NR, NR, T2, ALU.mult)
                ts(C1, C1, 1.0, ALU.add)
                tt(C1, C1, both(aa), ALU.mult)
                tt(C1, C1, T2, ALU.mult)
                tt(C2, BN2, both(OM), ALU.mult)
                tt(C2, C2, T2, ALU.mult)
                c1, d1, c2, d2 = C1[:, 0, :], C1[:, 1, :], C2[:, 0, :], C2[:, 1, :]
                X2, Y2 = NR[:, 0, :], NR[:, 1, :]
                ht, hr = HY[:, 0, :], HY[:, 1, :]
                tt(U1, d1, ss, ALU.mult)
                tt(U2, d2, hr, ALU.mult)
                tt(U1, U1, U2, ALU.add)
                tt(U1, U1, c1, ALU.mult)
                tt(U2, d1, ht, ALU.mult)
                tt(U3, d2, TR, ALU.mult)
                tt(U2, U2, U3, ALU.add)
                tt(U2, U2, c2, ALU.mult)
                tt(XY, U1, U2, ALU.add)
                stt(MM, XY, 2.0, Y2, ALU.mult, ALU.add)
                tt(DD, X2, Y2, ALU.mult)
                stt(DD, XY, 2.0, DD, ALU.mult, ALU.add)
                ts(DD, DD, 1.0, ALU.add)
                ts(DC, DD, MIN_NORM, ALU.max)
                recip(DC, DC)
                tt(U1, MM, X2, ALU.add)
                tt(U1, U1, DD, ALU.mult)
                tt(U1, U1, DC, ALU.mult)
                tt(U1, U1, DC, ALU.mult)
                ts(U1, U1, 0.0, ALU.max)
                V.tensor_copy(U2, U1)
                ask(m, base, 2)
                ts(U1, U1, MIN_NORM, ALU.max)
                recip(U1, U1)
                ts(U1, U1, MAX_NORM, ALU.mult, 1.0, ALU.min)
                tt(U2, U2, U1, ALU.mult)
                tt(U2, U2, U1, ALU.mult)
                tt(DC, DC, U1, ALU.mult)
                ts(MM, MM, 1.0, ALU.add)
                tt(MM, MM, DC, ALU.mult)
                ts(U3, X2, -1.0, ALU.mult, 1.0, ALU.add)
                tt(U3, U3, DC, ALU.mult)
                tt(E1, MM, c1, ALU.mult)
                tt(DC, U3, d1, ALU.mult)
                tt(E1, E1, DC, ALU.add)
                tt(E2, MM, c2, ALU.mult)
                tt(E3, U3, d2, ALU.mult)
                tt(MM, E1, ss, ALU.mult)
                tt(DC, E2, ht, ALU.mult)
                tt(MM, MM, DC, ALU.add)
                tt(DC, E3, hr, ALU.mult)
                tt(MM, MM, DC, ALU.add)
                tt(MM, MM, aa, ALU.mult)
                ts(U3, MM, -2.0, ALU.mult)
                tt(MM, U3, U2, ALU.add)
                tt(DD, U2, pp, ALU.mult)
                tt(DD, DD, U3, ALU.add)
                ts(DD, DD, 1.0, ALU.add)
                ts(DC, DD, MIN_NORM, ALU.max)
                recip(DC, DC)
                tt(U1, MM, pp, ALU.add)
                tt(U1, U1, DD, ALU.mult)
                tt(U1, U1, DC, ALU.mult)
                tt(U1, U1, DC, ALU.mult)
                ts(SQ[:, 0, :], U1, 1e-6, ALU.max)
                ts(MM, MM, 1.0, ALU.add)
                tt(MM, MM, aa, ALU.mult)
                tt(U3, E1, OM, ALU.mult)
                tt(E1, U3, MM, ALU.subtract)
                tt(E2, E2, OM, ALU.mult)
                tt(E3, E3, OM, ALU.mult)
                stt(U3, TR, 2.0, YY[:, 0, :], ALU.mult, ALU.add)
                tt(U3, U3, YY[:, 1, :], ALU.add)
                ts(SQ[:, 1, :], U3, 1e-24, ALU.max)
                ask(m, base, 3)
                ts(U1, SQ[:, 0, :], ARTANH_MAX, ALU.min)
                ts(U2, U1, -1.0, ALU.mult, 1.0, ALU.add)
                recip(U2, U2)
                ts(U1, U1, 1.0, ALU.add)
                tt(U1, U1, U2, ALU.mult)
                recip(SQ, SQ)
                ask(m, base, 4)
                ts(U1, U1, 0.5, ALU.mult)
                tt(U1, U1, SQ[:, 0, :], ALU.mult)
                tt(U1, U1, KC, ALU.mult)
                tt(U1, U1, DC, ALU.mult)
                tt(E1, E1, U1, ALU.mult)
                tt(E2, E2, U1, ALU.mult)
                tt(E3, E3, U1, ALU.mult)
                stt(E2, SQ[:, 1, :], 1e-7, E2, ALU.mult, ALU.add)
                stt(E3, SQ[:, 1, :], 1e-7, E3, ALU.mult, ALU.add)
                V.tensor_tensor(head[:, :, 0:D], head[:, :, 0:D], over(E1, D), ALU.mult)
                V.tensor_tensor(t_[:, :, 0:D], t_[:, :, 0:D], over(E2, D), ALU.mult)
                V.tensor_tensor(rel[:, :, 0:D], rel[:, :, 0:D], over(E3, D), ALU.mult)
                dve.drain()
                tt(head[:, :, 0:D], head[:, :, 0:D], t_[:, :, 0:D], ALU.add)
                tt(head[:, :, 0:D], head[:, :, 0:D], rel[:, :, 0:D], ALU.add)
                V.tensor_copy(msg[:, :, W - 1], pay[:, h, :, 3].bitcast(FP32))
                dve.drain().then_inc(S["asked", m], 1)

            def run_pass(m):
                hyp = m < 2
                V.memset(acc[:, :, :], 0.0)
                dve.drain()
                dve.sem_inc(S["rows_free", m], 2)
                dve.sem_inc(S["accumulated", m], 2)
                with dve.Fori(0, ITERS) as i:
                    for h in range(2):
                        await_reg(dve, "dve", S["loaded", m][h], 16 * i + 16)
                        V.tensor_tensor(onehot[:, h, :, :], over(pay[:, h, :, 1], P),
                                        iota[:, :].unsqueeze(1).to_broadcast([P, G, P]), ALU.is_equal)
                        if hyp:
                            V.tensor_tensor(type_hot[:, :, :], over(pay[:, h, :, 2], R),
                                            iota[:, 1:R + 1].unsqueeze(1).to_broadcast([P, G, R]), ALU.is_equal)
                        dve.drain().then_inc(S["hot_made", m], 1)
                        await_reg(dve, "dve", S["gathered", m][h], (i + 1) * (G * 16))
                        if hyp:
                            await_reg(dve, "dve", S["fetch_copied", m], (2 * i + h) * QG + (QG + 2))
                            messages(m, h, i)
                        for q in range(QG):
                            if q % 2 == 0:
                                dve.load(regs, rowoff[0:1, 0, bass.ds((2 * i + h) * G + 4 * q, 8)])
                            await_reg(dve, "dve", S["scattered", m], (2 * i + h) * QG + (q + 1))
                            for j in range(4):
                                b = dve.snap(regs[4 * (q % 2) + j], min_val=0, max_val=(NB - 1) * W)
                                V.tensor_tensor(flat_acc[:, bass.ds(b, W)], flat_acc[:, bass.ds(b, W)],
                                                ps_sum[q % 2][:, j * W:j * W + W], ALU.add)
                                if j < 3:
                                    dve.drain()
                            dve.drain().then_inc(S["accumulated", m], 1)
                        dve.sem_inc(S["rows_free", m], 1)
                meet(dve, BN[f"pass{m}"])

            def hop(k, n0):
                ts(stat[:, 2, :], acc[:, :, D], 1.0, ALU.max)
                recip(stat[:, 2, :], stat[:, 2, :])
                tt(acc[:, :, 0:D], acc[:, :, 0:D], over(stat[:, 2, :], D), ALU.mult)
                squares(acc[:, :, 0:D], stat[:, 0, :])
                dve.drain().then_inc(S["norms_asked", k], 1)
                dve.wait_ge(S["norms_done", k], n0)
                ts(stat[:, 1, :], stat[:, 1, :], 1e-12, ALU.max)
                recip(stat[:, 2, :], stat[:, 1, :])
                tt(acc[:, :, 0:D], acc[:, :, 0:D], over(stat[:, 2, :], D), ALU.mult)

            def layernorm(v, ask_s, done_s, done_n):
                rsum(stat[:, 2, :], v)
                ts(stat[:, 2, :], stat[:, 2, :], 1.0 / D, ALU.mult)
                tt(v, v, over(stat[:, 2, :], D), ALU.subtract)
                squares(v, stat[:, 0, :])
                ts(stat[:, 0, :], stat[:, 0, :], 1.0 / D, ALU.mult, LN_EPS, ALU.add)
                dve.drain().then_inc(ask_s, 1)
                dve.wait_ge(done_s, done_n)
                recip(stat[:, 1, :], stat[:, 1, :])
                tt(xs[:, :, :], v, over(stat[:, 1, :], D), ALU.mult)

            prepare(0)
            meet(dve, BN["prep0"])
            run_pass(0)
            V.tensor_copy(degree[:, :, :], acc[:, :, D:W])
            hop(0, 3)
            V.tensor_copy(tab[:, :, 0:D], acc[:, :, 0:D])
            dve.drain()
            prepare(1)
            meet(dve, BN["hop0"])
            run_pass(1)
            hop(1, 3)
            stt(acc[:, :, 0:D], tab[:, :, 0:D], 0.5, acc[:, :, 0:D], ALU.mult, ALU.add)
            stt(acc[:, :, 0:D], xs[:, :, :], 1.25, acc[:, :, 0:D], ALU.mult, ALU.add)
            layernorm(acc[:, :, 0:D], S["norms_asked", 1], S["norms_done", 1], 4)
            V.memset(rows[:, :, :, D:W], 1.0)
            meet(dve, BN["hop1"])
            meet(dve, BN["tab2"])

            def gru(t):
                s = 10 + t
                xin = xs if t == 0 else y
                V.memset(st_hT[D:D + 1, :, :], 1.0)
                V.memset(st_x[:, :, D:D + 1], 1.0)
                dve.drain()
                with dve.Fori(0, NITERS) as i:
                    bl = bass.ds(i * KB, KB)
                    V.tensor_copy(st_x[:, :, 0:D], xin[:, bl, :])
                    V.tensor_copy(st_x[:, :, D + 1:D + 3], degree[:, bl, :])
                    V.tensor_copy(st_u[:, :, 0:D], acc[:, bl, 0:D])
                    dve.drain()
                    V.tensor_tensor(st_u[:, :, D:P], st_x[:, :, 0:D], st_x[:, :, D + 1:D + 2].to_broadcast([P, KB, D]), ALU.mult)
                    dve.drain().then_inc(S["blk_staged", s], 1)
                    await_reg(dve, "dve", S["blk_act", s], 2 * i + 1)
                    tt(st_g[:, :, P + D:256], st_g[:, :, P + D:256], st_g[:, :, 0:D], ALU.mult)
                    tt(st_g[:, :, P:P + D], st_g[:, :, P:P + D], st_g[:, :, P + D:256], ALU.add)
                    dve.drain().then_inc(S["blk_act2", s], 1)
                    await_reg(dve, "dve", S["blk_act", s], 2 * i + 2)
                    tt(st_x[:, :, 0:D], st_x[:, :, 0:D], st_g[:, :, D:P], ALU.mult)
                    ts(st_g[:, :, D:P], st_g[:, :, D:P], -1.0, ALU.mult, 1.0, ALU.add)
                    tt(st_o, st_o, st_g[:, :, D:P], ALU.mult)
                    V.tensor_tensor(y[:, bl, :], st_o, st_x[:, :, 0:D], ALU.add)
                    dve.drain().then_inc(S["blk_back", s], 1)
                if t == 1:
                    tt(y, y, xs[:, :, :], ALU.add)
                    layernorm(y, S["blk_act2", s], S["blk_act", s], 2 * NITERS + 1)
                    dve.drain().then_inc(S["blk_back", s], 1)
                V.memset(rows[:, :, :, D:W], 1.0)

            def conv_a(l):
                s = 12 + l
                ts(stat[:, 4, :], acc[:, :, D], 1.0, ALU.max)
                recip(stat[:, 4, :], stat[:, 4, :])
                tt(acc[:, :, 0:D], acc[:, :, 0:D], over(stat[:, 4, :], D), ALU.mult)
                with dve.Fori(0, NITERS) as i:
                    bl = bass.ds(i * KB, KB)
                    V.tensor_copy(st_u[:, :, 0:D], acc[:, bl, 0:D])
                    V.tensor_copy(st_u[:, :, D:P], xs[:, bl, :])
                    dve.drain().then_inc(S["blk_staged", s], 1)
                    await_reg(dve, "dve", S["blk_made", s], i + 1)
                    for b, w in ((0, 4), (4, KB - 4)):
                        v = bank[4 + b // 4][:, 0:w * P].rearrange("p (b c) -> p b c", c=P)
                        V.tensor_copy(big[:, bass.ds(i * KB + b, w), :], v[:, :, 0:D])
                        V.tensor_copy(y[:, bass.ds(i * KB + b, w), :], v[:, :, D:P])
                    dve.drain().then_inc(S["blk_back", s], 1)

            def conv_b(l):
                s = 12 + l
                tt(acc[:, :, 0:D], acc[:, :, 0:D], over(stat[:, 4, :], D), ALU.mult)
                tt(y, y, acc[:, :, 0:D], ALU.add)
                tt(y, y, b_c2[:, l, :].unsqueeze(1).to_broadcast([P, NB, D]), ALU.add)
                tt(y, y, xs[:, :, :], ALU.add)
                layernorm(y, S["blk_act2", s], S["blk_act", s], 1)
                dve.drain().then_inc(S["blk_back", s], 1)
                V.memset(rows[:, :, :, D:W], 1.0)

            run_pass(2)
            gru(0)
            meet(dve, BN["gru0"])
            run_pass(3)
            gru(1)
            meet(dve, BN["gru1"])
            for l in range(2):
                run_pass(4 + 2 * l)
                conv_a(l)
                meet(dve, BN[f"c{l}a"])
                V.memset(rows[:, :, :, D:W], 1.0)
                dve.drain()
                run_pass(5 + 2 * l)
                conv_b(l)
                meet(dve, BN[f"c{l}b"])


def kernel(**inputs):
    import numpy as _np
    import concourse.bacc as _bacc
    from concourse import mybir as _mybir
    from concourse.bass_utils import run_bass_kernel_spmd as _run

    x = {k: _np.ascontiguousarray(v) for k, v in inputs.items()}
    for k in ("src", "dst", "edge_type_33", "edge_weight1"):
        x[k] = x[k].reshape(EP, EC)
    x["relT"] = x["L0_gnn_relation_emb"].T
    x["msg_WT"] = x.pop("L1_gnn_msg_W").transpose(0, 2, 1)
    x["WihT"] = x.pop("L1_gnn_gru_Wih").transpose(0, 2, 1)
    x["WhhT"] = x.pop("L1_gnn_gru_Whh").transpose(0, 2, 1)
    for w in ("W1_l", "W1_r", "W2_l", "W2_r"):
        x[f"L3_{w}T"] = x.pop(f"L3_gnn_{w}").T
    x["L2_b1c"] = x.pop("L2_gnn_b1").reshape(-1, 1)
    x["L3_b1c"] = x.pop("L3_gnn_b1").reshape(-1, 1)
    x["iota"] = _np.tile(_np.arange(P, dtype=_np.float32), (P, 1))
    x["ident"] = _np.eye(P, dtype=_np.float32)
    nc = _bacc.Bacc("TRN2", target_bir_lowering=False, num_devices=1)
    arrays, aps = {}, {}
    for name, v in x.items():
        v = _np.ascontiguousarray(v)
        arrays[f"in_{name}"] = v
        aps[name] = nc.dram_tensor(f"in_{name}", v.shape, _mybir.dt.from_np(v.dtype), kind="ExternalInput").ap()
    out = nc.dram_tensor("out_0", (N, D), _mybir.dt.float32, kind="ExternalOutput").ap()
    build(nc, aps, out)
    r = _run(nc, [arrays], core_ids=[0])
    return r.results[0]["out_0"]
```

```python
import concourse.bass as bass
from concourse import mybir
from contextlib import ExitStack

FP32 = mybir.dt.float32
BF16 = mybir.dt.bfloat16
I32 = mybir.dt.int32
I16 = mybir.dt.int16
ALU = mybir.AluOpType
ACT = mybir.ActivationFunctionType
AX = mybir.AxisListType

P = 128
D = 64
N = 12500
NB = -(-N // P)
LAST = N - (NB - 1) * P
E = 200000
EP, EC = 125, E // 125
R = 32
G = 32
QG = G // 4
GROUPS = 52
TILES = GROUPS * G
assert TILES >= E // P + NB and GROUPS % 2 == 0
ITERS = GROUPS // 2
W = D + 2
TW = 100
C_EE, C_NE, C_A, C_PP = 96, 97, 98, 99
RW = D + 2
CH = 5
HC = 40
NCH = HC // CH
GITERS = EC // HC // 2
KB = 7
NITERS = NB // KB
assert NITERS * KB == NB
MIN_NORM = 1e-15
MAX_NORM = 1.0 - 0.004
ARTANH_MAX = 1.0 - 1e-7
LN_EPS = 1e-5
PASSES = 8
AHEAD = (2, 2)
SLOTS = 56


def build(nc, a, out):
    ctx = ExitStack()
    with ctx:
        def sb(name, shape, dt=FP32):
            return ctx.enter_context(nc.sbuf_tensor(name, shape, dt))

        def sem(name):
            return ctx.enter_context(nc.semaphore(name))

        payload = [nc.dram_tensor(f"payload_{k}", (TILES * P, 4), I32, kind="Internal").ap() for k in ("src", "dst")]
        block_rows = [nc.dram_tensor(f"block_rows_{k}", (2, TILES), I16, kind="Internal").ap() for k in ("src", "dst")]
        table_hyp = nc.dram_tensor("table_hyp", (NB * P, TW), FP32, kind="Internal").ap()
        table_lin = nc.dram_tensor("table_lin", (NB * P, D), FP32, kind="Internal").ap()

        xs = sb("xs", [P, NB, D])
        acc = sb("acc", [P, NB, W])
        tab = sb("tab", [P, NB, TW])
        rows = sb("rows", [P, 2, G, TW])
        onehot = sb("onehot", [P, 2, G, P])
        head0 = sb("head0", [P, G, TW])
        rel0 = sb("rel0", [P, G, RW])
        msg = sb("msg", [P, G, W])
        type_hot = sb("type_hot", [P, 2, G, R])
        sel_t = sb("sel_t", [P, 2, 4 * P])
        type_t = sb("type_t", [P, 2, P])
        pay = sb("pay", [P, 2, G, 4], I32)
        sc = sb("sc", [P, SLOTS, G])
        rowoff = sb("rowoff", [1, 2, TILES], I16)
        degree = sb("degree", [P, NB, 2])
        stat = sb("stat", [P, 6, NB])
        iota = sb("iota", [P, P])
        ident = sb("ident", [P, P])
        iota_bf = sb("iota_bf", [P, NB], BF16)
        before = sb("before", [P, P], BF16)
        notbefore = sb("notbefore", [P, P], BF16)
        ones_bf = sb("ones_bf", [P, P], BF16)
        relT = sb("relT", [D, R])
        relblk = sb("relblk", [P, 4, RW])

        flat_x = xs[:, :, :].rearrange("p b d -> p (b d)")
        head = [head0[:, :, :], flat_x[:, 0:G * TW].rearrange("p (t c) -> p t c", c=TW)]
        rel = [rel0[:, :, :], flat_x[:, G * TW:G * (TW + RW)].rearrange("p (t c) -> p t c", c=RW)]
        flat_rel = rel0[:, :, :].rearrange("p t c -> p (t c)")
        w_c1 = flat_rel[:, 0:2 * P].rearrange("p (l c) -> p l c", l=2)
        w_c2 = flat_rel[:, 2 * P:4 * P].rearrange("p (l c) -> p l c", l=2)
        w_cnt = flat_rel[0:D + 3, 6 * P:7 * P].rearrange("p (t c) -> p t c", t=2)
        b_c1 = flat_rel[:, 4 * P:4 * P + 2]
        b_c2 = flat_rel[:, 5 * P:6 * P].rearrange("p (l c) -> p l c", l=2)
        flat_head = head0[:, :, :].rearrange("p t c -> p (t c)")
        w_msg = flat_head[:, 0:2 * D].rearrange("p (t d) -> p t d", t=2)
        w_ih = flat_head[0:D + 1, 2 * D:8 * D].rearrange("p (t d) -> p t d", t=2)
        w_hh = flat_head[0:D + 1, 8 * D:14 * D].rearrange("p (t d) -> p t d", t=2)
        flat_rows = rows[:, :, :, :].rearrange("p a b c -> p (a b c)")
        big = flat_rows[:, 0:NB * D].rearrange("p (b d) -> p b d", d=D)
        y = tab[:, :, :].rearrange("p a b -> p (a b)")[:, 0:NB * D].rearrange("p (b d) -> p b d", d=D)
        flat_hot = onehot[:, :, :, :].rearrange("p a b c -> p (a b c)")
        hist = flat_hot.bitcast(BF16)[0:EP, 0:2 * HC * NB].rearrange("p (h c b) -> p h c b", h=2, b=NB)
        flat_tab = tab[:, :, :].rearrange("p a b -> p (a b)")
        edges_in = flat_tab.bitcast(I32)[0:EP, 0:4 * EC].rearrange("p (k c) -> p k c", k=4)
        stage = flat_rows.bitcast(I32)[0:EP, 0:2 * HC * 4].rearrange("p (h c k) -> p h c k", h=2, k=4)
        keyf = flat_rows.bitcast(BF16)[0:EP, 800:800 + EC]
        addr = flat_rows.bitcast(I32)[0:EP, 2100:2100 + 2 * HC].rearrange("p (h c) -> p h c", h=2)
        posf = flat_rows[0:EP, 2200:2200 + HC]
        posi = flat_rows.bitcast(I32)[0:EP, 2250:2250 + 4 * HC].rearrange("p (k c) -> p k c", k=4)
        picked = flat_rows[0:EP, 2500:2500 + CH * NB].rearrange("p (c b) -> p c b", b=NB)
        start_f = flat_rows[:, 3000:3000 + CH * NB].rearrange("p (c b) -> p c b", b=NB)
        count_f = flat_rows[:, 3500:3500 + CH * NB].rearrange("p (c b) -> p c b", b=NB)
        bucket = flat_rows[:, 4000:4000 + 6 * NB].rearrange("p (k b) -> p k b", b=NB)
        bucket_i = flat_rows.bitcast(I32)[:, 4600:4600 + 2 * NB].rearrange("p (k b) -> p k b", b=NB)
        TPP = TILES // P
        tile_no = flat_rows[:, 4800:4800 + TPP]
        tile_blk = flat_rows[:, 4820:4820 + TPP]
        tile_off = flat_rows.bitcast(I16)[:, 2 * 4840:2 * 4840 + 2 * TPP].rearrange("p (k t) -> p k t", k=2)
        tile_cmp = flat_rows[:, 4900:4900 + TPP * NB].rearrange("p (t b) -> p t b", b=NB)
        fill = msg[:, :, :].rearrange("p a b -> p (a b)").bitcast(I32)[:, 0:G * 4].rearrange("p (t k) -> p t k", k=4)

        hot = flat_hot
        def part(width, at=[0]):
            v = hot[:, at[0]:at[0] + KB * width].rearrange("p (b c) -> p b c", c=width)
            at[0] += KB * width
            return v

        st_us, st_xs = [part(P), part(P)], [part(D + 3), part(D + 3)]
        st_uT, st_xT, st_hT, st_g, st_o = part(P), part(P), part(P), part(256), part(D)
        st_u = st_us[0]

        bank = [ctx.enter_context(nc.psum_tensor(f"bank{i}", [P, 512], FP32)) for i in range(8)]
        ps_sel, ps_rel, ps_head, ps_sum = bank[0:2], bank[2:4], bank[4:6], bank[6:8]
        ps_type = [b[:, 3 * P:4 * P] for b in ps_sum]

        tick = {k: sem(f"tick_{k}") for k in ("sp", "pool", "dve", "act", "pe")}
        arrived = sem("arrived")
        loads = sem("loads")
        stores = sem("stores")
        cleared = sem("cleared")
        x_again = sem("x_again")
        S = {}
        for k in range(2):
            for n in ("hist_counted", "start_ready", "ranked", "rank_read", "staged", "hot_ready"):
                S[n, k] = sem(f"{n}_{k}")
            S["sent", k] = [sem(f"sent_{k}_{h}") for h in range(2)]
            for n in ("norms_asked", "norms_done", "q_staged", "q_transposed", "q_copied", "q_made", "q_kept"):
                S[n, k] = sem(f"{n}_{k}")
        for n in range(PASSES):
            S["loaded", n] = [sem(f"loaded_{n}_{h}") for h in range(2)]
            S["gathered", n] = [sem(f"gathered_{n}_{h}") for h in range(2)]
            for m in ("hot_made", "rows_free", "accumulated", "scattered"):
                S[m, n] = sem(f"{m}_{n}")
            if n < 2:
                for m in ("transposed", "sel_copied", "fetched", "fetch_copied", "asked", "answered", "coefficients", "mixed"):
                    S[m, n] = sem(f"{m}_{n}")
        for n in range(4):
            for m in ("blk_staged", "blk_transposed", "blk_copied", "blk_mid", "blk_mid_kept", "blk_made", "blk_act", "blk_act2", "blk_back"):
                S[m, n + 10] = sem(f"{m}_{n}")

        block = ctx.enter_context(nc.Block())
        EPB = 5

        def over(v, w):
            return v.unsqueeze(2).to_broadcast([v.shape[0], v.shape[1], w])

        def meet(eng, k):
            eng.drain().then_inc(arrived, 1)
            eng.wait_ge(arrived, EPB * k)

        def await_reg(eng, who, s, v):
            eng.wait_ge(s, v)
            eng.sem_inc(tick[who], 1)

        pv = [p.rearrange("(g q t) k -> g q t k", q=P, t=G) for p in payload]

        B_CONST, B_G = 1, [2, 3]
        b_next = 4
        BN = {}
        for name in ("x", "prep0", "pass0", "hop0", "pass1", "hop1", "tab2", "pass2", "gru0", "pass3", "gru1",
                     "pass4", "c0a", "pass5", "c0b", "pass6", "c1a", "pass7", "c1b"):
            BN[name] = b_next
            b_next += 1

        slot = iter(range(SLOTS))

        def run(n):
            q = [next(slot) for _ in range(n)][0]
            return sc[:, q:q + n, :]

        NN, YY, Q4, RN, T1, T2, BB, CC, CN, NR, DN, RD = (run(n) for n in (2, 2, 4, 2, 2, 2, 2, 4, 2, 2, 2, 2))
        PA, PB, MS, EW, EO, SQ, RS = (run(n) for n in (2, 2, 2, 4, 4, 2, 2))
        OM, KC, XY, DD, DC, U1, U2, U3, A1, B1 = (run(1)[:, 0, :] for _ in range(10))

        @block.sync
        def _(sp):
            n = 0
            for k, name in enumerate(("src", "dst", "edge_type_33")):
                sp.dma_start(edges_in[:, k, :], a[name]).then_inc(loads, 16)
                n += 1
            sp.dma_start(edges_in[:, 3, :].bitcast(FP32), a["edge_weight1"]).then_inc(loads, 16)
            for t, name in ((iota, "iota"), (ident, "ident")):
                sp.dma_start(t[:, :], a[name]).then_inc(loads, 16)
            sp.dma_start(relT[:, :], a["relT"]).then_inc(loads, 16)
            n += 4
            sp.wait_ge(cleared, 1)
            for j in range(4):
                sp.dma_start(relblk[R * j:R * j + R, j, 0:D], a["L0_gnn_relation_emb"]).then_inc(loads, 16)
                n += 1
            sp.dma_start(xs[:, 0:NB - 1, :], a["x"][0:(NB - 1) * P, :].rearrange("(b p) d -> p b d", p=P)).then_inc(loads, 16)
            sp.dma_start(xs[0:LAST, NB - 1, :], a["x"][(NB - 1) * P:N, :]).then_inc(loads, 16)
            n += 2
            sp.wait_ge(cleared, 2)
            with sp.Fori(0, GROUPS) as g:
                for k in range(2):
                    sp.dma_start(pv[k][bass.ds(g, 1)].rearrange("a q t k -> (a q) t k"), fill).then_inc(stores, 16)
            sp.wait_ge(stores, 2 * GROUPS * 16)
            sp.wait_ge(loads, n * 16)
            meet(sp, B_CONST)
            stored = 2 * GROUPS * 16
            for k in range(2):
                sp.wait_ge(S["start_ready", k], 1)
                sp.dma_start(block_rows[k].rearrange("k (p t) -> p k t", p=P), tile_off).then_inc(stores, 16)
                stored += 16
                sp.wait_ge(stores, stored)
                meet(sp, B_G[k])
            meet(sp, BN["x"])

            def load_rowoff(k):
                nonlocal n
                sp.dma_start(rowoff[0:1, :, :].rearrange("p k t -> p (k t)"),
                             block_rows[k].rearrange("k t -> (k t)").unsqueeze(0)).then_inc(loads, 16)
                n += 1
                sp.wait_ge(loads, n * 16)

            def run_pass(m, k):
                with sp.Fori(0, ITERS) as i:
                    for h in range(2):
                        await_reg(sp, "sp", S["rows_free", m], 2 * i + (h + 1))
                        sp.dma_start(pay[:, h, :, :],
                                     pv[k][bass.ds(2 * i + h, 1)].rearrange("a q t k -> (a q) t k")).then_inc(S["loaded", m][h], 16)
                sp.wait_ge(S["loaded", m][1], ITERS * 16)
                sp.wait_ge(S["loaded", m][0], ITERS * 16)
                meet(sp, BN[f"pass{m}"])

            def store_table(dst, srcv):
                nonlocal stored
                sp.dma_start(dst.rearrange("(b p) c -> p b c", p=P), srcv).then_inc(stores, 16)
                stored += 16
                sp.wait_ge(stores, stored)

            load_rowoff(0)
            sp.wait_ge(S["q_kept", 0], NITERS)
            store_table(table_hyp, tab[:, :, :])
            meet(sp, BN["prep0"])
            run_pass(0, 0)
            sp.wait_ge(S["q_kept", 1], NITERS)
            store_table(table_hyp, tab[:, :, :])
            meet(sp, BN["hop0"])
            run_pass(1, 0)
            sp.wait_ge(cleared, 3)
            sp.dma_start(xs[:, 0:NB - 1, :], a["x"][0:(NB - 1) * P, :].rearrange("(b p) d -> p b d", p=P)).then_inc(x_again, 16)
            sp.dma_start(xs[0:LAST, NB - 1, :], a["x"][(NB - 1) * P:N, :]).then_inc(x_again, 16)
            for t in range(2):
                sp.dma_start(w_cnt[D + 1:D + 2, t, :], a["L1_gnn_msg_b"][t:t + 1, :]).then_inc(x_again, 16)
                sp.dma_start(w_cnt[D + 2:D + 3, t, :], a["msg_WT"][t, 2 * D:2 * D + 1, :]).then_inc(x_again, 16)
                sp.dma_start(w_msg[:, t, :], a["msg_WT"][t, 0:2 * D, :]).then_inc(x_again, 16)
                sp.dma_start(w_ih[0:D, t, :], a["WihT"][t]).then_inc(x_again, 16)
                sp.dma_start(w_ih[D:D + 1, t, :], a["L1_gnn_gru_bih"][t:t + 1, :]).then_inc(x_again, 16)
                sp.dma_start(w_hh[0:D, t, :], a["WhhT"][t]).then_inc(x_again, 16)
                sp.dma_start(w_hh[D:D + 1, t, :], a["L1_gnn_gru_bhh"][t:t + 1, :]).then_inc(x_again, 16)
            for l, (h, names) in enumerate(((16, ("L2_gnn_W1_l", "L2_gnn_W1_r", "L2_gnn_W2_l", "L2_gnn_W2_r", "L2_b1c")),
                                            (128, ("L3_W1_lT", "L3_W1_rT", "L3_W2_lT", "L3_W2_rT", "L3_b1c")))):
                sp.dma_start(w_c1[0:D, l, 0:h], a[names[0]]).then_inc(x_again, 16)
                sp.dma_start(w_c1[D:P, l, 0:h], a[names[1]]).then_inc(x_again, 16)
                sp.dma_start(w_c2[0:h, l, 0:D], a[names[2]]).then_inc(x_again, 16)
                sp.dma_start(w_c2[0:h, l, D:P], a[names[3]]).then_inc(x_again, 16)
                sp.dma_start(b_c1[0:h, l:l + 1], a[names[4]]).then_inc(x_again, 16)
            sp.dma_start(b_c2[:, 0, :], a["L2_gnn_b2"].partition_broadcast(P)).then_inc(x_again, 16)
            sp.dma_start(b_c2[:, 1, :], a["L3_gnn_b2"].partition_broadcast(P)).then_inc(x_again, 16)
            meet(sp, BN["hop1"])
            store_table(table_lin, xs[:, :, :])
            meet(sp, BN["tab2"])
            run_pass(2, 0)
            sp.wait_ge(S["blk_back", 10], NITERS + 1)
            store_table(table_lin, y)
            meet(sp, BN["gru0"])
            run_pass(3, 0)
            sp.wait_ge(S["blk_back", 11], NITERS + 2)
            store_table(table_lin, xs[:, :, :])
            load_rowoff(1)
            meet(sp, BN["gru1"])
            for l in range(2):
                run_pass(4 + 2 * l, 1)
                sp.wait_ge(S["blk_back", 12 + l], NITERS)
                store_table(table_lin, big)
                meet(sp, BN[f"c{l}a"])
                run_pass(5 + 2 * l, 1)
                if l == 0:
                    sp.wait_ge(S["blk_back", 12], NITERS + 1)
                    store_table(table_lin, xs[:, :, :])
                    meet(sp, BN["c0b"])
                else:
                    sp.wait_ge(S["blk_back", 13], NITERS + 1)
                    sp.dma_start(out[0:(NB - 1) * P, :].rearrange("(b p) d -> p b d", p=P), xs[:, 0:NB - 1, :]).then_inc(stores, 16)
                    sp.dma_start(out[(NB - 1) * P:N, :], xs[0:LAST, NB - 1, :]).then_inc(stores, 16)
                    stored += 32
                    sp.wait_ge(stores, stored)
                    meet(sp, BN["c1b"])

        @block.gpsimd
        def _(pool):
            meet(pool, B_CONST)
            for k in range(2):
                sent = S["sent", k]
                with pool.Fori(0, GITERS) as i:
                    for h in range(2):
                        await_reg(pool, "pool", S["staged", k], 2 * i + (h + 1))
                        for c in range(HC):
                            pool.indirect_dma_start(
                                out=payload[k][:, :], out_offset=bass.IndirectOffsetOnAxis(ap=addr[:, h, c:c + 1], axis=0),
                                in_=stage[:, h, c, :], in_offset=None).then_inc(sent[h], 16)
                for h in range(2):
                    pool.wait_ge(sent[h], GITERS * HC * 16)
                meet(pool, B_G[k])
            meet(pool, BN["x"])
            meet(pool, BN["prep0"])

            def gather(m, i, h):
                table, width = (table_hyp, TW) if m < 2 else (table_lin, D)
                await_reg(pool, "pool", S["loaded", m][h], 16 * i + 16)
                await_reg(pool, "pool", S["rows_free", m], 2 * i + (h + 1))
                for t in range(G):
                    pool.indirect_dma_start(
                        out=rows[:, h, t, 0:width], out_offset=None, in_=table[:, :],
                        in_offset=bass.IndirectOffsetOnAxis(ap=pay[:, h, t, 0:1], axis=0)).then_inc(S["gathered", m][h], 16)

            def mix(m, g, h):
                hd, rl = head[h][:, :, 0:D], rel[h][:, :, 0:D]
                await_reg(pool, "pool", S["coefficients", m], g + 1)
                nc.gpsimd.tensor_tensor(rl, rl, over(EO[:, 3, :], D), ALU.mult).then_inc(S["mixed", m], 1)
                await_reg(pool, "pool", S["mixed", m], 2 * g + 1)
                await_reg(pool, "pool", S["rows_free", m], g + 3)
                nc.gpsimd.tensor_tensor(hd, hd, rl, ALU.add).then_inc(S["mixed", m], 1)

            def run_pass(m):
                if m < 2:
                    gather(m, 0, 0)
                    gather(m, 0, 1)
                    with pool.Fori(0, ITERS - 1) as i:
                        for h in range(2):
                            mix(m, 2 * i + h, h)
                            gather(m, i + 1, h)
                    mix(m, GROUPS - 2, 0)
                    mix(m, GROUPS - 1, 1)
                else:
                    with pool.Fori(0, ITERS) as i:
                        for h in range(2):
                            gather(m, i, h)
                for h in range(2):
                    pool.wait_ge(S["gathered", m][h], ITERS * G * 16)
                meet(pool, BN[f"pass{m}"])

            run_pass(0)
            meet(pool, BN["hop0"])
            run_pass(1)
            meet(pool, BN["hop1"])
            meet(pool, BN["tab2"])
            run_pass(2)
            meet(pool, BN["gru0"])
            run_pass(3)
            meet(pool, BN["gru1"])
            for l in range(2):
                run_pass(4 + 2 * l)
                meet(pool, BN[f"c{l}a"])
                run_pass(5 + 2 * l)
                meet(pool, BN[f"c{l}b"])

        @block.tensor
        def _(pe):
            meet(pe, B_CONST)
            for k in range(2):
                totals = bank[0]

                def count(h, first):
                    for c in range(NCH):
                        last = nc.tensor.matmul(totals[:, 0:CH * NB], ones_bf[0:EP, :],
                                                hist[:, h, c * CH:c * CH + CH, :].rearrange("p c b -> p (c b)"),
                                                start=first and c == 0, stop=False, skip_group_check=True)
                    last.then_inc(S["hist_counted", k], 1)
                for h in range(2):
                    pe.wait_ge(S["hot_ready", k], h + 1)
                    count(h, h == 0)
                with pe.Fori(0, GITERS - 1) as i:
                    for h in range(2):
                        await_reg(pe, "pe", S["hot_ready", k], 2 * i + (h + 3))
                        count(h, False)
                place = bank[1]
                pe.wait_ge(S["start_ready", k], 1)
                nc.tensor.matmul(place[0:EP, 0:CH * NB], ident[:, 0:EP], start_f.rearrange("p c b -> p (c b)"),
                                 start=True, stop=False, skip_group_check=True)
                with pe.Fori(0, GITERS) as i:
                    for h in range(2):
                        await_reg(pe, "pe", S["hot_ready", k], 2 * i + (h + 1 + 2 * GITERS))
                        for c in range(NCH):
                            hot_c = hist[:, h, c * CH:c * CH + CH, :].rearrange("p c b -> p (c b)")
                            nc.tensor.matmul(place[0:EP, 0:CH * NB], before[0:EP, 0:EP], hot_c,
                                             start=False, stop=False, skip_group_check=True).then_inc(S["ranked", k], 1)
                            await_reg(pe, "pe", S["rank_read", k], (2 * i + h) * NCH + (c + 1))
                            nc.tensor.matmul(place[0:EP, 0:CH * NB], notbefore[0:EP, 0:EP], hot_c,
                                             start=False, stop=False, skip_group_check=True)
                meet(pe, B_G[k])
            meet(pe, BN["x"])

            def make_q(k):
                with pe.Fori(0, NITERS) as i:
                    await_reg(pe, "pe", S["q_staged", k], i + 1)
                    for j in range(KB):
                        last = nc.tensor.transpose(bank[j // 4][0:D, (j % 4) * P:(j % 4) * P + P], st_u[:, j, 0:D], ident[:, :])
                    last.then_inc(S["q_transposed", k], 1)
                    await_reg(pe, "pe", S["q_copied", k], i + 1)
                    for j in range(KB):
                        last = nc.tensor.matmul(bank[2][:, j * R:j * R + R], st_uT[0:D, j, :], relT[:, :], start=True, stop=True)
                    last.then_inc(S["q_made", k], 1)

            regs = [pe.alloc_register(f"head_block_{j}") for j in range(4)]

            def turn(m, g, h, q):
                for j in range(4):
                    nc.tensor.transpose(ps_sel[q % 2][:, j * P:j * P + P], onehot[:, h, 4 * q + j, :], ident[:, :])
                nc.tensor.transpose(ps_type[q % 2], type_hot[:, h, 4 * q:4 * q + 4, :].rearrange("p a b -> p (a b)"),
                                    ident[:, :]).then_inc(S["transposed", m], 1)

            def fetch(m, g, h, q):
                pe.load(regs, rowoff[0:1, 1, bass.ds(g * G + 4 * q, 4)])
                await_reg(pe, "pe", S["fetch_copied", m], g * QG + (q + 1))
                await_reg(pe, "pe", S["sel_copied", m], g * QG + (q + 1))
                for j in range(4):
                    b = pe.snap(regs[j], min_val=0, max_val=(NB - 1) * TW)
                    nc.tensor.matmul(ps_head[q % 2][:, j * TW:j * TW + TW], sel_t[:, q % 2, j * P:j * P + P],
                                     flat_tab[:, bass.ds(b, TW)], start=True, stop=True)
                nc.tensor.matmul(ps_rel[q % 2][:, 0:4 * RW], type_t[:, q % 2, :],
                                 relblk[:, :, :].rearrange("p a b -> p (a b)"),
                                 start=True, stop=True).then_inc(S["fetched", m], 1)

            def fetch_group(m, g, h):
                await_reg(pe, "pe", S["hot_made", m], g + 1)
                turn(m, g, h, 0)
                for q in range(1, QG):
                    turn(m, g, h, q)
                    fetch(m, g, h, q - 1)
                fetch(m, g, h, QG - 1)

            def sum_group(m, g, h):
                hyp = m < 2
                if hyp:
                    await_reg(pe, "pe", S["answered", m], 5 * g + 5)
                for q in range(QG):
                    await_reg(pe, "pe", S["accumulated", m], g * QG + (q + 1))
                    for j in range(4):
                        t = 4 * q + j
                        mv = head[h][:, t, 0:W] if hyp else rows[:, h, t, 0:W]
                        last = nc.tensor.matmul(ps_sum[q % 2][:, j * W:j * W + W], onehot[:, h, t, :], mv, start=True, stop=True)
                    last.then_inc(S["scattered", m], 1)

            def run_pass(m):
                if m < 2:
                    fetch_group(m, 0, 0)
                    with pe.Fori(0, ITERS - 1) as i:
                        fetch_group(m, 2 * i + 1, 1)
                        sum_group(m, 2 * i, 0)
                        fetch_group(m, 2 * i + 2, 0)
                        sum_group(m, 2 * i + 1, 1)
                    fetch_group(m, GROUPS - 1, 1)
                    sum_group(m, GROUPS - 2, 0)
                    sum_group(m, GROUPS - 1, 1)
                else:
                    with pe.Fori(0, ITERS) as i:
                        for h in range(2):
                            await_reg(pe, "pe", S["hot_made", m], 2 * i + (h + 1))
                            await_reg(pe, "pe", S["gathered", m][h], (i + 1) * (G * 16))
                            sum_group(m, 2 * i + h, h)
                meet(pe, BN[f"pass{m}"])

            def gru(t):
                s = 10 + t

                def turn_blocks(step, h):
                    await_reg(pe, "pe", S["blk_staged", s], step + 1)
                    for j in range(KB):
                        nc.tensor.transpose(bank[j // 4][:, (j % 4) * P:(j % 4) * P + P], st_us[h][:, j, :], ident[:, :])
                    for j in range(KB):
                        last = nc.tensor.transpose(bank[2 + j // 4][0:D + 3, (j % 4) * P:(j % 4) * P + P], st_xs[h][:, j, :], ident[:, :])
                    last.then_inc(S["blk_transposed", s], 1)

                def gates(step):
                    await_reg(pe, "pe", S["blk_copied", s], step + 1)
                    for j in range(KB):
                        o = bank[4 + j // 4][0:D, (j % 4) * P:(j % 4) * P + P]
                        nc.tensor.matmul(o, w_msg[:, t, :], st_uT[:, j, :], start=True, stop=False)
                        last = nc.tensor.matmul(o, w_cnt[:, t, :], st_xT[0:D + 3, j, :], start=False, stop=True)
                    last.then_inc(S["blk_mid", s], 1)
                    await_reg(pe, "pe", S["blk_mid_kept", s], step + 1)
                    for j in range(KB):
                        bk, o = bank[4 + j // 2], (j % 2) * 256
                        nc.tensor.matmul(bk[:, o:o + P], st_hT[0:D + 1, j, :], w_ih[:, t, 0:P], start=True, stop=False)
                        nc.tensor.matmul(bk[:, o:o + P], st_xT[0:D + 1, j, :], w_hh[:, t, 0:P], start=False, stop=True)
                        nc.tensor.matmul(bk[:, o + P:o + P + D], st_hT[0:D + 1, j, :], w_ih[:, t, P:3 * D], start=True, stop=True)
                        last = nc.tensor.matmul(bk[:, o + P + D:o + 256], st_xT[0:D + 1, j, :], w_hh[:, t, P:3 * D], start=True, stop=True)
                    last.then_inc(S["blk_made", s], 1)

                turn_blocks(0, 0)
                with pe.Fori(0, NITERS // 2 - 1) as i:
                    gates(2 * i)
                    turn_blocks(2 * i + 1, 1)
                    gates(2 * i + 1)
                    turn_blocks(2 * i + 2, 0)
                gates(NITERS - 2)
                turn_blocks(NITERS - 1, 1)
                gates(NITERS - 1)

            def conv(l):
                s = 12 + l
                with pe.Fori(0, NITERS) as i:
                    await_reg(pe, "pe", S["blk_staged", s], i + 1)
                    for j in range(KB):
                        last = nc.tensor.transpose(bank[j // 4][:, (j % 4) * P:(j % 4) * P + P], st_u[:, j, :], ident[:, :])
                    last.then_inc(S["blk_transposed", s], 1)
                    await_reg(pe, "pe", S["blk_copied", s], i + 1)
                    for j in range(KB):
                        last = nc.tensor.matmul(bank[2 + j // 4][:, (j % 4) * P:(j % 4) * P + P], w_c1[:, l, :], st_uT[:, j, :],
                                                start=True, stop=True)
                    last.then_inc(S["blk_mid", s], 1)
                    await_reg(pe, "pe", S["blk_mid_kept", s], i + 1)
                    for j in range(KB):
                        last = nc.tensor.matmul(bank[4 + j // 4][:, (j % 4) * P:(j % 4) * P + P], st_hT[:, j, :], w_c2[:, l, :],
                                                start=True, stop=True)
                    last.then_inc(S["blk_made", s], 1)

            make_q(0)
            meet(pe, BN["prep0"])
            run_pass(0)
            make_q(1)
            meet(pe, BN["hop0"])
            run_pass(1)
            meet(pe, BN["hop1"])
            meet(pe, BN["tab2"])
            run_pass(2)
            gru(0)
            meet(pe, BN["gru0"])
            run_pass(3)
            gru(1)
            meet(pe, BN["gru1"])
            for l in range(2):
                run_pass(4 + 2 * l)
                conv(l)
                meet(pe, BN[f"c{l}a"])
                run_pass(5 + 2 * l)
                meet(pe, BN[f"c{l}b"])

        @block.scalar
        def _(act):
            meet(act, B_CONST)
            for k in range(2):
                meet(act, B_G[k])
            meet(act, BN["x"])

            def norms(k):
                act.wait_ge(S["norms_asked", k], 1)
                if k == 0:
                    nc.scalar.activation(relblk[:, :, D + 1], relblk[:, :, D], ACT.Sqrt)
                nc.scalar.activation(stat[:, 1, :], stat[:, 0, :], ACT.Sqrt).then_inc(S["norms_done", k], 1)
                act.wait_ge(S["norms_asked", k], 2)
                nc.scalar.activation(stat[:, 2, :], stat[:, 1, :], ACT.Tanh).then_inc(S["norms_done", k], 1)

            def make_q(k):
                with act.Fori(0, NITERS) as i:
                    await_reg(act, "act", S["q_transposed", k], i + 1)
                    nc.scalar.copy(st_uT[0:D, 0:4, :], bank[0][0:D, :].rearrange("p (b c) -> p b c", c=P))
                    nc.scalar.copy(st_uT[0:D, 4:KB, :], bank[1][0:D, 0:(KB - 4) * P].rearrange("p (b c) -> p b c", c=P)
                                   ).then_inc(S["q_copied", k], 1)

            def run_pass(m):
                if m >= 2:
                    meet(act, BN[f"pass{m}"])
                    return
                act.sem_inc(S["fetch_copied", m], 2)

                def steps(g, h):
                    def copy_sel(q):
                        await_reg(act, "act", S["transposed", m], g * QG + (q + 1))
                        nc.scalar.copy(sel_t[:, q % 2, :], ps_sel[q % 2][:, :])
                        nc.scalar.copy(type_t[:, q % 2, :], ps_type[q % 2]).then_inc(S["sel_copied", m], 1)

                    def copy_fetch(q):
                        await_reg(act, "act", S["fetched", m], g * QG + (q + 1))
                        nc.scalar.copy(head[h][:, 4 * q:4 * q + 4, :].rearrange("p a b -> p (a b)"), ps_head[q % 2][:, 0:4 * TW])
                        nc.scalar.copy(rel[h][:, 4 * q:4 * q + 4, :].rearrange("p a b -> p (a b)"),
                                       ps_rel[q % 2][:, 0:4 * RW]).then_inc(S["fetch_copied", m], 1)
                    copy_sel(0)
                    for q in range(1, QG):
                        copy_sel(q)
                        copy_fetch(q - 1)
                        yield
                    copy_fetch(QG - 1)
                    yield

                def answer(g, h, n, o, iv, f):
                    await_reg(act, "act", S["asked", m], 4 * g + n)
                    nc.scalar.activation(o, iv, f).then_inc(S["answered", m], 1)

                def group(g, h, ahead):
                    answer(g, h, 1, T1, T1, ACT.Tanh)
                    for _ in range(AHEAD[0]):
                        next(ahead, None)
                    answer(g, h, 2, U1, U2, ACT.Sqrt)
                    for _ in range(AHEAD[1]):
                        next(ahead, None)
                    answer(g, h, 3, SQ, SQ, ACT.Sqrt)
                    answer(g, h, 4, A1, A1, ACT.Ln)
                    for _ in ahead:
                        pass
                    await_reg(act, "act", S["mixed", m], 2 * g + 2)
                    nc.scalar.activation(head[h][:, :, 0:D], head[h][:, :, 0:D], ACT.Relu).then_inc(S["answered", m], 1)

                for _ in steps(0, 0):
                    pass
                with act.Fori(0, ITERS - 1) as i:
                    group(2 * i, 0, steps(2 * i + 1, 1))
                    group(2 * i + 1, 1, steps(2 * i + 2, 0))
                group(GROUPS - 2, 0, steps(GROUPS - 1, 1))
                group(GROUPS - 1, 1, iter(()))
                meet(act, BN[f"pass{m}"])

            def root(k, c):
                act.wait_ge(S["norms_asked", k], c)
                nc.scalar.activation(stat[:, 1, :], stat[:, 0, :], ACT.Sqrt).then_inc(S["norms_done", k], 1)

            norms(0)
            make_q(0)
            meet(act, BN["prep0"])
            run_pass(0)
            root(0, 3)
            norms(1)
            make_q(1)
            meet(act, BN["hop0"])
            run_pass(1)
            root(1, 3)
            root(1, 4)
            meet(act, BN["hop1"])
            meet(act, BN["tab2"])

            def copy_turned(s, both):
                nc.scalar.copy(st_uT[:, 0:4, :], bank[0][:, :].rearrange("p (b c) -> p b c", c=P))
                last = nc.scalar.copy(st_uT[:, 4:KB, :], bank[1][:, 0:(KB - 4) * P].rearrange("p (b c) -> p b c", c=P))
                if both:
                    nc.scalar.copy(st_xT[0:D + 3, 0:4, :], bank[2][0:D + 3, :].rearrange("p (b c) -> p b c", c=P))
                    last = nc.scalar.copy(st_xT[0:D + 3, 4:KB, :], bank[3][0:D + 3, 0:(KB - 4) * P].rearrange("p (b c) -> p b c", c=P))
                last.then_inc(S["blk_copied", s], 1)

            def gru(t):
                s = 10 + t

                def turned(step):
                    await_reg(act, "act", S["blk_transposed", s], step + 1)
                    copy_turned(s, True)

                def gates(step, more):
                    await_reg(act, "act", S["blk_mid", s], step + 1)
                    nc.scalar.copy(st_hT[0:D, 0:4, :], bank[4][0:D, :].rearrange("p (b c) -> p b c", c=P))
                    nc.scalar.copy(st_hT[0:D, 4:KB, :], bank[5][0:D, 0:(KB - 4) * P].rearrange("p (b c) -> p b c", c=P)
                                   ).then_inc(S["blk_mid_kept", s], 1)
                    await_reg(act, "act", S["blk_made", s], step + 1)
                    await_reg(act, "act", S["blk_back", s], step + 1)
                    for b in range(4):
                        w = min(2, KB - 2 * b)
                        v = bank[4 + b][:, 0:w * 256].rearrange("p (b c) -> p b c", c=256)
                        nc.scalar.activation(st_g[:, 2 * b:2 * b + w, 0:P], v[:, :, 0:P], ACT.Sigmoid)
                        last = nc.scalar.copy(st_g[:, 2 * b:2 * b + w, P:256], v[:, :, P:256])
                    last.then_inc(S["blk_act", s], 1)
                    if more:
                        turned(step + 1)
                    await_reg(act, "act", S["blk_act2", s], step + 1)
                    nc.scalar.activation(st_o[:, :, :], st_g[:, :, P:P + D], ACT.Tanh).then_inc(S["blk_act", s], 1)

                turned(0)
                with act.Fori(0, NITERS // 2 - 1) as i:
                    gates(2 * i, True)
                    gates(2 * i + 1, True)
                gates(NITERS - 2, True)
                gates(NITERS - 1, False)
                if t == 1:
                    act.wait_ge(S["blk_act2", s], NITERS + 1)
                    nc.scalar.activation(stat[:, 1, :], stat[:, 0, :], ACT.Sqrt).then_inc(S["blk_act", s], 1)

            def conv(l):
                s = 12 + l
                with act.Fori(0, NITERS) as i:
                    await_reg(act, "act", S["blk_transposed", s], i + 1)
                    copy_turned(s, False)
                    await_reg(act, "act", S["blk_mid", s], i + 1)
                    nc.scalar.activation(st_hT[:, 0:4, :], bank[2][:, :].rearrange("p (b c) -> p b c", c=P), ACT.Relu, bias=b_c1[:, l:l + 1])
                    nc.scalar.activation(st_hT[:, 4:KB, :], bank[3][:, 0:(KB - 4) * P].rearrange("p (b c) -> p b c", c=P), ACT.Relu,
                                         bias=b_c1[:, l:l + 1]).then_inc(S["blk_mid_kept", s], 1)

            run_pass(2)
            gru(0)
            meet(act, BN["gru0"])
            run_pass(3)
            gru(1)
            meet(act, BN["gru1"])
            for l in range(2):
                run_pass(4 + 2 * l)
                conv(l)
                meet(act, BN[f"c{l}a"])
                run_pass(5 + 2 * l)
                act.wait_ge(S["blk_act2", 12 + l], 1)
                nc.scalar.activation(stat[:, 1, :], stat[:, 0, :], ACT.Sqrt).then_inc(S["blk_act", 12 + l], 1)
                meet(act, BN[f"c{l}b"])

        @block.vector
        def _(dve):
            V = nc.vector

            def tt(o, x, y_, op, last=True):
                r = V.tensor_tensor(o, x, y_, op)
                if last:
                    dve.drain()
                return r

            def ts(o, x, c1, op1, c2=None, op2=None):
                if op2 is None:
                    V.tensor_scalar(o, x, c1, None, op1)
                else:
                    V.tensor_scalar(o, x, c1, c2, op1, op2)
                dve.drain()

            def stt(o, x, c, y_, o1, o2):
                V.scalar_tensor_tensor(out=o, in0=x, scalar=c, in1=y_, op0=o1, op1=o2)
                dve.drain()

            def recip(o, x):
                V.reciprocal(o, x)
                dve.drain()

            def rsum(o, x):
                V.reduce_sum(o, x, axis=AX.X)
                dve.drain()

            for t in (relblk,):
                V.memset(t[:], 0.0)
            V.memset(xs[64:128, NB - 1, :], 0.0)
            dve.drain().then_inc(cleared, 1)
            V.memset(fill[:, :, 0:1], 0)
            V.memset(fill[:, :, 1:2], -1)
            V.memset(fill[:, :, 2:3], 1)
            V.memset(fill[:, :, 3:4], 0)
            dve.drain().then_inc(cleared, 1)
            V.memset(ones_bf[:, :], 1.0)
            dve.drain()
            meet(dve, B_CONST)
            V.tensor_copy(iota_bf[:, :], iota[:, 0:NB])
            tt(start_f.rearrange("p c b -> p (c b)")[:, 0:P], ident[:, :], iota[:, :], ALU.mult)
            rsum(stat[:, 0, 0:1], start_f.rearrange("p c b -> p (c b)")[:, 0:P])
            V.tensor_scalar(before[:, :], iota[:, :], stat[:, 0, 0:1], None, ALU.is_gt)
            V.tensor_scalar(notbefore[:, :], iota[:, :], stat[:, 0, 0:1], None, ALU.is_le)
            V.tensor_scalar(bucket[:, 0, 0:1], stat[:, 0, 0:1], float(TPP), None, ALU.mult)
            TY = keyf
            V.tensor_copy(TY, edges_in[:, 2, :])
            dve.drain()
            V.tensor_scalar(tile_no, iota[:, 0:TPP], bucket[:, 0, 0:1], None, ALU.add)
            ty0 = hist[:, 0, :, :].rearrange("p c b -> p (c b)")[:, 0:EC]
            ts(ty0, TY, 0.0, ALU.is_equal)
            stt(TY, ty0, float(R), TY, ALU.mult, ALU.add)
            V.tensor_copy(edges_in[:, 2, :], TY)
            V.tensor_copy(stat[:, 5, 0:TPP], tile_no)
            dve.drain()

            def make_hist(h, c0):
                V.tensor_tensor(hist[:, h, :, :], over(keyf[:, bass.ds(c0, HC)], NB),
                                iota_bf[0:EP, :].unsqueeze(1).to_broadcast([EP, HC, NB]), ALU.is_equal)

            for k in range(2):
                key = edges_in[:, k, :]
                tmpi = flat_rows.bitcast(I32)[0:EP, 2500:2500 + EC]
                V.tensor_scalar(tmpi, key, 7, None, ALU.arith_shift_right)
                dve.drain()
                V.tensor_copy(keyf, tmpi)
                dve.drain()
                for h in range(2):
                    make_hist(h, h * HC)
                    dve.drain().then_inc(S["hot_ready", k], 1)
                with dve.Fori(0, GITERS - 1) as i:
                    for h in range(2):
                        await_reg(dve, "dve", S["hist_counted", k], 2 * i + (h + 1))
                        make_hist(h, i * (2 * HC) + (h + 2) * HC)
                        dve.drain().then_inc(S["hot_ready", k], 1)
                dve.wait_ge(S["hist_counted", k], 2 * GITERS)
                V.tensor_copy(count_f.rearrange("p c b -> p (c b)"), bank[0][:, 0:CH * NB])
                dve.drain()
                rsum(bucket[:, 1, :], count_f.rearrange("p c b -> p b c"))
                ts(bucket[:, 2, :], bucket[:, 1, :], float(P - 1), ALU.add)
                V.tensor_copy(bucket_i[:, 0, :], bucket[:, 2, :])
                dve.drain()
                V.tensor_scalar(bucket_i[:, 1, :], bucket_i[:, 0, :], 7, None, ALU.arith_shift_right)
                dve.drain()
                V.tensor_copy(bucket[:, 2, :], bucket_i[:, 1, :])
                V.memset(bucket[:, 3, :], 1.0)
                dve.drain()
                V.tensor_tensor_scan(bucket[:, 4, :], bucket[:, 3, :], bucket[:, 2, :], 0.0, ALU.mult, ALU.add)
                dve.drain()
                tt(bucket[:, 5, :], bucket[:, 4, :], bucket[:, 2, :], ALU.subtract)
                ts(start_f[:, 0, :], bucket[:, 5, :], float(P), ALU.mult)
                for c in range(1, CH):
                    tt(start_f[:, c, :], start_f[:, c - 1, :], count_f[:, c - 1, :], ALU.add)
                tt(tile_cmp, over(stat[:, 5, 0:TPP], NB), bucket[:, 4, :].unsqueeze(1).to_broadcast([P, TPP, NB]), ALU.is_ge)
                rsum(tile_blk, tile_cmp)
                ts(tile_blk, tile_blk, float(NB - 1), ALU.min)
                V.tensor_scalar(tile_off[:, 0, :], tile_blk, float(W), None, ALU.mult)
                V.tensor_scalar(tile_off[:, 1, :], tile_blk, float(TW), None, ALU.mult)
                dve.drain().then_inc(S["start_ready", k], 1)
                with dve.Fori(0, GITERS) as i:
                    for h in range(2):
                        c0 = i * (2 * HC) + h * HC
                        make_hist(h, c0)
                        dve.drain().then_inc(S["hot_ready", k], 1)
                        await_reg(dve, "dve", S["sent", k][h], i * (HC * 16))
                        V.tensor_copy(stage[:, h, :, 0], edges_in[:, 1 - k, bass.ds(c0, HC)])
                        V.tensor_scalar(stage[:, h, :, 1], edges_in[:, k, bass.ds(c0, HC)], P - 1, None, ALU.bitwise_and)
                        V.tensor_copy(stage[:, h, :, 2], edges_in[:, 2, bass.ds(c0, HC)])
                        V.tensor_copy(stage[:, h, :, 3].bitcast(FP32), edges_in[:, 3, bass.ds(c0, HC)].bitcast(FP32))
                        dve.drain()
                        for c in range(NCH):
                            await_reg(dve, "dve", S["ranked", k], (2 * i + h) * NCH + (c + 1))
                            V.tensor_tensor(picked, bank[1][0:EP, 0:CH * NB].rearrange("p (c b) -> p c b", b=NB),
                                            hist[:, h, c * CH:c * CH + CH, :], ALU.mult).then_inc(S["rank_read", k], 1)
                            dve.drain()
                            rsum(posf[:, c * CH:c * CH + CH], picked)
                        V.tensor_copy(posi[:, 0, :], posf)
                        dve.drain()
                        V.tensor_scalar(posi[:, 1, :], posi[:, 0, :], P - 1, 5, ALU.bitwise_and, ALU.logical_shift_left)
                        V.tensor_scalar(posi[:, 2, :], posi[:, 0, :], 7, G - 1, ALU.arith_shift_right, ALU.bitwise_and)
                        V.tensor_scalar(posi[:, 3, :], posi[:, 0, :], -(P * G), None, ALU.bitwise_and)
                        dve.drain()
                        V.tensor_tensor(posi[:, 1, :], posi[:, 1, :], posi[:, 2, :], ALU.bitwise_or)
                        dve.drain()
                        V.tensor_tensor(addr[:, h, :], posi[:, 1, :], posi[:, 3, :], ALU.bitwise_or)
                        dve.drain().then_inc(S["staged", k], 1)
                meet(dve, B_G[k])

            tt(big[:, 0:4, :], relblk[:, :, 0:D], relblk[:, :, 0:D], ALU.mult)
            rsum(relblk[:, :, D], big[:, 0:4, :])
            V.tensor_copy(tab[:, :, 0:D], xs[:, :, :])
            V.memset(msg[:, :, D:W], 1.0)
            V.memset(rows[:, :, :, D:W], 1.0)
            meet(dve, BN["x"])

            def squares(v, o):
                tt(big, v, v, ALU.mult)
                rsum(o, big)

            def prepare(k):
                squares(tab[:, :, 0:D], tab[:, :, C_EE])
                V.tensor_copy(stat[:, 0, :], tab[:, :, C_EE])
                dve.drain().then_inc(S["norms_asked", k], 1)
                dve.wait_ge(S["norms_done", k], 1)
                ts(stat[:, 1, :], stat[:, 1, :], MIN_NORM, ALU.max)
                dve.drain().then_inc(S["norms_asked", k], 1)
                dve.wait_ge(S["norms_done", k], 2)
                recip(stat[:, 3, :], stat[:, 1, :])
                tt(stat[:, 4, :], stat[:, 2, :], stat[:, 3, :], ALU.mult)
                V.tensor_copy(tab[:, :, C_NE], stat[:, 1, :])
                V.tensor_copy(tab[:, :, C_A], stat[:, 4, :])
                tt(stat[:, 3, :], stat[:, 4, :], stat[:, 4, :], ALU.mult)
                tt(tab[:, :, C_PP], stat[:, 3, :], stat[:, 0, :], ALU.mult)
                with dve.Fori(0, NITERS) as i:
                    V.tensor_copy(st_u[:, :, 0:D], tab[:, bass.ds(i * KB, KB), 0:D])
                    dve.drain().then_inc(S["q_staged", k], 1)
                    await_reg(dve, "dve", S["q_made", k], i + 1)
                    V.tensor_copy(tab[:, bass.ds(i * KB, KB), D:D + R], bank[2][:, 0:KB * R].rearrange("p (b c) -> p b c", c=R))
                    dve.drain().then_inc(S["q_kept", k], 1)

            regs = [dve.alloc_register(f"sum_block_{j}") for j in range(16)]
            flat_acc = acc[:, :, :].rearrange("p a b -> p (a b)")

            def ask(m):
                dve.drain().then_inc(S["asked", m], 1)

            def answered(m, g, n):
                await_reg(dve, "dve", S["answered", m], 5 * g + n)

            def both(v):
                return v.unsqueeze(1).to_broadcast([P, 2, G])

            def four(v):
                return v.unsqueeze(1).to_broadcast([P, 4, G])

            def messages(m, g, h, between, meanwhile):
                t_, hd, rl, hot_ = rows[:, h, :, :], head[h], rel[h], type_hot[:, h, :, :]
                prod = msg[:, :, 0:D]
                ss, aa, pp = hd[:, :, C_EE], hd[:, :, C_A], hd[:, :, C_PP]
                TT, TS, STT, level = V.tensor_tensor, V.tensor_scalar, V.scalar_tensor_tensor, dve.drain
                MUL, ADD, SUB, MAX = ALU.mult, ALU.add, ALU.subtract, ALU.max
                SH, HY, RT = Q4[:, 0:2, :], Q4[:, 1:3, :], Q4[:, 2:4, :]
                C1, C2 = CC[:, 0:2, :], CC[:, 2:4, :]
                c1, d1, c2, d2 = (CC[:, k, :] for k in range(4))
                c12, d12 = CC[:, 0:3:2, :], CC[:, 1:4:2, :]
                X2, Y2 = NR[:, 0, :], NR[:, 1, :]

                def ttl(o, x, y_, op):
                    TT(o, x, y_, op)
                    level()

                V.tensor_copy(NN[:, 0, :], t_[:, :, C_NE])
                TS(NN[:, 1, :], rl[:, :, D + 1], MIN_NORM, None, MAX)
                V.tensor_copy(YY[:, 0, :], t_[:, :, C_EE])
                V.tensor_copy(YY[:, 1, :], rl[:, :, D])
                V.tensor_copy(Q4[:, 0, :], ss)
                TS(OM, pp, -1.0, 1.0, MUL, ADD)
                level()
                ttl(prod, hd[:, :, 0:D], t_[:, :, 0:D], MUL)
                V.reduce_sum(Q4[:, 1, :], prod, axis=AX.X)
                level()
                TT(prod[:, :, 0:R], hd[:, :, D:D + R], hot_, MUL)
                TT(prod[:, :, R:2 * R], t_[:, :, D:D + R], hot_, MUL)
                level()
                V.reduce_sum(RT, prod.rearrange("p t (k r) -> p k t r", k=2), axis=AX.X)
                between()
                V.reciprocal(RN, NN)
                TS(KC, OM, MIN_NORM, None, MAX)
                level()
                V.reciprocal(DC, KC)
                level()
                TT(T1, NN, both(DC), MUL)
                ask(m)
                meanwhile()
                TT(U3, YY[:, 0, :], YY[:, 1, :], ADD)
                answered(m, g, 1)
                ttl(BB, T1, RN, MUL)
                TT(T1, BB, BB, MUL)
                TT(T2, BB, HY, MUL)
                TT(CN, BB, both(OM), MUL)
                level()
                TT(T1, T1, YY, MUL)
                TT(T2, T2, both(aa), MUL)
                STT(out=U3, in0=Q4[:, 3, :], scalar=2.0, in1=U3, op0=MUL, op1=ADD)
                level()
                STT(out=BB, in0=T2, scalar=2.0, in1=T1, op0=MUL, op1=ADD)
                TT(DN, T1, both(pp), MUL)
                TS(SQ[:, 1, :], U3, 1e-24, None, MAX)
                level()
                STT(out=DN, in0=T2, scalar=2.0, in1=DN, op0=MUL, op1=ADD)
                TT(NR, BB, both(pp), ADD)
                STT(out=C1, in0=BB, scalar=1.0, in1=both(aa), op0=ADD, op1=MUL)
                level()
                TS(RD, DN, 1.0, MIN_NORM, ADD, MAX)
                STT(out=NR, in0=DN, scalar=1.0, in1=NR, op0=ADD, op1=MUL)
                level()
                V.reciprocal(RD, RD)
                level()
                TT(NR, NR, RD, MUL)
                TT(C1, C1, RD, MUL)
                TT(C2, CN, RD, MUL)
                level()
                TT(NR, NR, RD, MUL)
                TT(PA, SH, both(d1), MUL)
                TT(PB, RT, both(d2), MUL)
                level()
                TT(PA, PA, PB, ADD)
                TT(DD, X2, Y2, MUL)
                TS(MS[:, 1, :], X2, -1.0, 1.0, MUL, ADD)
                level()
                ttl(PA, PA, c12, MUL)
                ttl(XY, PA[:, 0, :], PA[:, 1, :], ADD)
                STT(out=A1, in0=XY, scalar=2.0, in1=Y2, op0=MUL, op1=ADD)
                STT(out=DD, in0=XY, scalar=2.0, in1=DD, op0=MUL, op1=ADD)
                level()
                TS(DC, DD, 1.0, MIN_NORM, ADD, MAX)
                TT(U1, A1, X2, ADD)
                TS(MS[:, 0, :], A1, 1.0, None, ADD)
                level()
                V.reciprocal(DC, DC)
                STT(out=U1, in0=DD, scalar=1.0, in1=U1, op0=ADD, op1=MUL)
                level()
                TT(U1, U1, DC, MUL)
                TT(MS, MS, both(DC), MUL)
                level()
                TT(U1, U1, DC, MUL)
                TT(EW[:, 0:2, :], c12, both(MS[:, 0, :]), MUL)
                TT(EW[:, 2:4, :], d12, both(MS[:, 1, :]), MUL)
                level()
                TS(U2, U1, 0.0, None, MAX)
                TT(EW[:, 0, :], EW[:, 0, :], EW[:, 2, :], ADD)
                ask(m)
                TT(PA, EW[:, 0:2, :], SH, MUL)
                TT(U3, EW[:, 3, :], Q4[:, 2, :], MUL)
                level()
                ttl(B1, PA[:, 0, :], PA[:, 1, :], ADD)
                ttl(B1, B1, U3, ADD)
                ttl(EW[:, 2, :], B1, aa, MUL)
                answered(m, g, 2)
                TS(U1, U1, MIN_NORM, None, MAX)
                level()
                V.reciprocal(U1, U1)
                level()
                TS(U1, U1, MAX_NORM, 1.0, MUL, ALU.min)
                level()
                TT(EW, EW, four(U1), MUL)
                TT(U2, U2, U1, MUL)
                level()
                TT(U2, U2, U1, MUL)
                TS(U3, EW[:, 2, :], -2.0, None, MUL)
                TT(EO, EW, four(OM), MUL)
                level()
                TT(A1, U3, U2, ADD)
                TT(DD, U2, pp, MUL)
                level()
                TT(DD, DD, U3, ADD)
                TT(U1, A1, pp, ADD)
                STT(out=B1, in0=A1, scalar=1.0, in1=aa, op0=ADD, op1=MUL)
                level()
                TS(DC, DD, 1.0, MIN_NORM, ADD, MAX)
                STT(out=U1, in0=DD, scalar=1.0, in1=U1, op0=ADD, op1=MUL)
                TT(EO[:, 0, :], EO[:, 0, :], B1, SUB)
                level()
                V.reciprocal(DC, DC)
                level()
                TT(U1, U1, DC, MUL)
                TT(KC, KC, DC, MUL)
                level()
                ttl(U1, U1, DC, MUL)
                TS(SQ[:, 0, :], U1, 1e-6, None, MAX)
                ask(m)
                TT(EO, EO, four(KC), MUL)
                answered(m, g, 3)
                TS(A1, SQ[:, 0, :], ARTANH_MAX, None, ALU.min)
                V.reciprocal(RS, SQ)
                level()
                TS(B1, A1, -1.0, 1.0, MUL, ADD)
                TS(U1, A1, 1.0, None, ADD)
                level()
                V.reciprocal(B1, B1)
                level()
                TT(A1, U1, B1, MUL)
                ask(m)
                TS(U2, RS[:, 1, :], 1e-7, None, MUL)
                TS(U3, RS[:, 0, :], 0.5, None, MUL)
                level()
                answered(m, g, 4)
                ttl(U3, U3, A1, MUL)
                ttl(EO, EO, four(U3), MUL)
                TT(EO[:, 1:4:2, :], EO[:, 1:4:2, :], both(U2), ADD)
                dve.drain().then_inc(S["coefficients", m], 1)
                TT(hd[:, :, 0:D], hd[:, :, 0:D], over(EO[:, 0, :], D), MUL)
                TT(t_[:, :, 0:D], t_[:, :, 0:D], over(EO[:, 1, :], D), MUL)
                V.memset(hd[:, :, D:D + 1], 1.0)
                V.tensor_copy(hd[:, :, D + 1], pay[:, h, :, 3].bitcast(FP32))
                level()
                TT(hd[:, :, 0:D], hd[:, :, 0:D], t_[:, :, 0:D], ADD)
                dve.drain().then_inc(S["rows_free", m], 1)

            def make_hot(m, i, h):
                await_reg(dve, "dve", S["loaded", m][h], 16 * i + 16)
                V.tensor_tensor(onehot[:, h, :, :], over(pay[:, h, :, 1], P),
                                iota[:, :].unsqueeze(1).to_broadcast([P, G, P]), ALU.is_equal)
                if m < 2:
                    V.tensor_tensor(type_hot[:, h, :, :], over(pay[:, h, :, 2], R),
                                    iota[:, 1:R + 1].unsqueeze(1).to_broadcast([P, G, R]), ALU.is_equal)
                dve.drain().then_inc(S["hot_made", m], 1)

            def add_sums(m, g):
                for q in range(QG):
                    if q % 4 == 0:
                        dve.load(regs, rowoff[0:1, 0, bass.ds(g * G + 4 * q, 16)])
                    await_reg(dve, "dve", S["scattered", m], g * QG + (q + 1))
                    for j in range(4):
                        b = dve.snap(regs[4 * (q % 4) + j], min_val=0, max_val=(NB - 1) * W)
                        V.tensor_tensor(flat_acc[:, bass.ds(b, W)], flat_acc[:, bass.ds(b, W)],
                                        ps_sum[q % 2][:, j * W:j * W + W], ALU.add)
                        if j < 3:
                            dve.drain()
                    dve.drain().then_inc(S["accumulated", m], 1)

            def hyp_group(m, i, h, between, meanwhile):
                await_reg(dve, "dve", S["gathered", m][h], (i + 1) * (G * 16))
                await_reg(dve, "dve", S["fetch_copied", m], (2 * i + h) * QG + (QG + 2))
                messages(m, 2 * i + h, h, between, meanwhile)

            def run_pass(m):
                V.memset(acc[:, :, :], 0.0)
                dve.drain()
                dve.sem_inc(S["rows_free", m], 2)
                dve.sem_inc(S["accumulated", m], 2)
                if m < 2:
                    make_hot(m, 0, 0)
                    hyp_group(m, 0, 0, lambda: None, lambda: make_hot(m, 0, 1))
                    with dve.Fori(0, ITERS - 1) as i:
                        hyp_group(m, i, 1, lambda: add_sums(m, 2 * i), lambda: make_hot(m, i + 1, 0))
                        hyp_group(m, i + 1, 0, lambda: add_sums(m, 2 * i + 1), lambda: make_hot(m, i + 1, 1))
                    hyp_group(m, ITERS - 1, 1, lambda: add_sums(m, GROUPS - 2), lambda: None)
                    add_sums(m, GROUPS - 1)
                else:
                    with dve.Fori(0, ITERS) as i:
                        for h in range(2):
                            make_hot(m, i, h)
                            await_reg(dve, "dve", S["gathered", m][h], (i + 1) * (G * 16))
                            add_sums(m, 2 * i + h)
                            dve.sem_inc(S["rows_free", m], 1)
                meet(dve, BN[f"pass{m}"])

            def hop(k, n0):
                ts(stat[:, 2, :], acc[:, :, D], 1.0, ALU.max)
                recip(stat[:, 2, :], stat[:, 2, :])
                tt(acc[:, :, 0:D], acc[:, :, 0:D], over(stat[:, 2, :], D), ALU.mult)
                squares(acc[:, :, 0:D], stat[:, 0, :])
                dve.drain().then_inc(S["norms_asked", k], 1)
                dve.wait_ge(S["norms_done", k], n0)
                ts(stat[:, 1, :], stat[:, 1, :], 1e-12, ALU.max)
                recip(stat[:, 2, :], stat[:, 1, :])
                tt(acc[:, :, 0:D], acc[:, :, 0:D], over(stat[:, 2, :], D), ALU.mult)

            def layernorm(v, ask_s, done_s, done_n):
                rsum(stat[:, 2, :], v)
                ts(stat[:, 2, :], stat[:, 2, :], 1.0 / D, ALU.mult)
                tt(v, v, over(stat[:, 2, :], D), ALU.subtract)
                squares(v, stat[:, 0, :])
                ts(stat[:, 0, :], stat[:, 0, :], 1.0 / D, ALU.mult, LN_EPS, ALU.add)
                dve.drain().then_inc(ask_s, 1)
                dve.wait_ge(done_s, done_n)
                recip(stat[:, 1, :], stat[:, 1, :])
                tt(xs[:, :, :], v, over(stat[:, 1, :], D), ALU.mult)

            prepare(0)
            meet(dve, BN["prep0"])
            run_pass(0)
            V.tensor_copy(degree[:, :, :], acc[:, :, D:W])
            hop(0, 3)
            V.tensor_copy(tab[:, :, 0:D], acc[:, :, 0:D])
            dve.drain()
            prepare(1)
            meet(dve, BN["hop0"])
            run_pass(1)
            V.memset(xs[64:128, NB - 1, :], 0.0)
            V.memset(flat_rel[:, 0:7 * P], 0.0)
            dve.drain().then_inc(cleared, 1)
            hop(1, 3)
            dve.wait_ge(x_again, 28 * 16)
            stt(acc[:, :, 0:D], tab[:, :, 0:D], 0.5, acc[:, :, 0:D], ALU.mult, ALU.add)
            stt(acc[:, :, 0:D], xs[:, :, :], 1.25, acc[:, :, 0:D], ALU.mult, ALU.add)
            layernorm(acc[:, :, 0:D], S["norms_asked", 1], S["norms_done", 1], 4)
            V.memset(rows[:, :, :, D:W], 1.0)
            meet(dve, BN["hop1"])
            meet(dve, BN["tab2"])

            def gru(t):
                s = 10 + t
                xin = xs if t == 0 else y
                dve.sem_inc(S["blk_back", s], 1)
                V.memset(st_hT[D:D + 1, :, :], 1.0)
                for h in range(2):
                    V.memset(st_xs[h][:, :, D:D + 1], 1.0)
                dve.drain()

                def stage_blocks(step, h):
                    bl, st_x, st_n = bass.ds(step * KB, KB), st_xs[h], st_us[h]
                    V.tensor_copy(st_x[:, :, 0:D], xin[:, bl, :])
                    V.tensor_copy(st_x[:, :, D + 1:D + 3], degree[:, bl, :])
                    V.tensor_copy(st_n[:, :, 0:D], acc[:, bl, 0:D])
                    dve.drain()
                    V.tensor_tensor(st_n[:, :, D:P], st_x[:, :, 0:D], st_x[:, :, D + 1:D + 2].to_broadcast([P, KB, D]), ALU.mult)
                    dve.drain().then_inc(S["blk_staged", s], 1)

                def finish(step, h):
                    bl, st_x = bass.ds(step * KB, KB), st_xs[h]
                    await_reg(dve, "dve", S["blk_act", s], 2 * step + 1)
                    tt(st_g[:, :, P + D:256], st_g[:, :, P + D:256], st_g[:, :, 0:D], ALU.mult)
                    tt(st_g[:, :, P:P + D], st_g[:, :, P:P + D], st_g[:, :, P + D:256], ALU.add)
                    dve.drain().then_inc(S["blk_act2", s], 1)
                    await_reg(dve, "dve", S["blk_act", s], 2 * step + 2)
                    tt(st_x[:, :, 0:D], st_x[:, :, 0:D], st_g[:, :, D:P], ALU.mult)
                    ts(st_g[:, :, D:P], st_g[:, :, D:P], -1.0, ALU.mult, 1.0, ALU.add)
                    tt(st_o, st_o, st_g[:, :, D:P], ALU.mult)
                    V.tensor_tensor(y[:, bl, :], st_o, st_x[:, :, 0:D], ALU.add)
                    dve.drain().then_inc(S["blk_back", s], 1)

                stage_blocks(0, 0)
                with dve.Fori(0, NITERS // 2 - 1) as i:
                    stage_blocks(2 * i + 1, 1)
                    finish(2 * i, 0)
                    stage_blocks(2 * i + 2, 0)
                    finish(2 * i + 1, 1)
                stage_blocks(NITERS - 1, 1)
                finish(NITERS - 2, 0)
                finish(NITERS - 1, 1)
                if t == 1:
                    tt(y, y, xs[:, :, :], ALU.add)
                    layernorm(y, S["blk_act2", s], S["blk_act", s], 2 * NITERS + 1)
                    dve.drain().then_inc(S["blk_back", s], 1)
                V.memset(rows[:, :, :, D:W], 1.0)

            def conv_a(l):
                s = 12 + l
                ts(stat[:, 4, :], acc[:, :, D], 1.0, ALU.max)
                recip(stat[:, 4, :], stat[:, 4, :])
                tt(acc[:, :, 0:D], acc[:, :, 0:D], over(stat[:, 4, :], D), ALU.mult)
                with dve.Fori(0, NITERS) as i:
                    bl = bass.ds(i * KB, KB)
                    V.tensor_copy(st_u[:, :, 0:D], acc[:, bl, 0:D])
                    V.tensor_copy(st_u[:, :, D:P], xs[:, bl, :])
                    dve.drain().then_inc(S["blk_staged", s], 1)
                    await_reg(dve, "dve", S["blk_made", s], i + 1)
                    for b, w in ((0, 4), (4, KB - 4)):
                        v = bank[4 + b // 4][:, 0:w * P].rearrange("p (b c) -> p b c", c=P)
                        V.tensor_copy(big[:, bass.ds(i * KB + b, w), :], v[:, :, 0:D])
                        V.tensor_copy(y[:, bass.ds(i * KB + b, w), :], v[:, :, D:P])
                    dve.drain().then_inc(S["blk_back", s], 1)

            def conv_b(l):
                s = 12 + l
                tt(acc[:, :, 0:D], acc[:, :, 0:D], over(stat[:, 4, :], D), ALU.mult)
                tt(y, y, acc[:, :, 0:D], ALU.add)
                tt(y, y, b_c2[:, l, :].unsqueeze(1).to_broadcast([P, NB, D]), ALU.add)
                tt(y, y, xs[:, :, :], ALU.add)
                layernorm(y, S["blk_act2", s], S["blk_act", s], 1)
                dve.drain().then_inc(S["blk_back", s], 1)
                V.memset(rows[:, :, :, D:W], 1.0)

            run_pass(2)
            gru(0)
            meet(dve, BN["gru0"])
            run_pass(3)
            gru(1)
            meet(dve, BN["gru1"])
            for l in range(2):
                run_pass(4 + 2 * l)
                conv_a(l)
                meet(dve, BN[f"c{l}a"])
                V.memset(rows[:, :, :, D:W], 1.0)
                dve.drain()
                run_pass(5 + 2 * l)
                conv_b(l)
                meet(dve, BN[f"c{l}b"])


def kernel(**inputs):
    import numpy as _np
    import concourse.bacc as _bacc
    from concourse import mybir as _mybir
    from concourse.bass_utils import run_bass_kernel_spmd as _run

    x = {k: _np.ascontiguousarray(v) for k, v in inputs.items()}
    for k in ("src", "dst", "edge_type_33", "edge_weight1"):
        x[k] = x[k].reshape(EP, EC)
    x["relT"] = x["L0_gnn_relation_emb"].T
    x["msg_WT"] = x.pop("L1_gnn_msg_W").transpose(0, 2, 1)
    x["WihT"] = x.pop("L1_gnn_gru_Wih").transpose(0, 2, 1)
    x["WhhT"] = x.pop("L1_gnn_gru_Whh").transpose(0, 2, 1)
    for w in ("W1_l", "W1_r", "W2_l", "W2_r"):
        x[f"L3_{w}T"] = x.pop(f"L3_gnn_{w}").T
    x["L2_b1c"] = x.pop("L2_gnn_b1").reshape(-1, 1)
    x["L3_b1c"] = x.pop("L3_gnn_b1").reshape(-1, 1)
    x["iota"] = _np.tile(_np.arange(P, dtype=_np.float32), (P, 1))
    x["ident"] = _np.eye(P, dtype=_np.float32)
    nc = _bacc.Bacc("TRN2", target_bir_lowering=False, num_devices=1)
    arrays, aps = {}, {}
    for name, v in x.items():
        v = _np.ascontiguousarray(v)
        arrays[f"in_{name}"] = v
        aps[name] = nc.dram_tensor(f"in_{name}", v.shape, _mybir.dt.from_np(v.dtype), kind="ExternalInput").ap()
    out = nc.dram_tensor("out_0", (N, D), _mybir.dt.float32, kind="ExternalOutput").ap()
    build(nc, aps, out)
    r = _run(nc, [arrays], core_ids=[0])
    return r.results[0]["out_0"]
```
